# Optimizing a Trainium2 kernel written in Bass

```python
import numpy as np
import jax
import jax.numpy as jnp

def _softmax(x, axis=-1):
    return jax.nn.softmax(x, axis=axis)

def _gelu(x):
    return jax.nn.gelu(x, approximate=True)

def _silu(x):
    return jax.nn.silu(x)

def _sigmoid(x):
    return jax.nn.sigmoid(x)

def _layernorm(x, axis=-1, eps=1e-05):
    m = jnp.mean(x, axis=axis, keepdims=True)
    v = jnp.var(x, axis=axis, keepdims=True)
    return (x - m) / jnp.sqrt(v + eps)

def _scatter_add(tgt, idx, src, axis=0):
    return tgt.at[idx].add(src)

def _segment_sum(src, seg, n):
    return jax.ops.segment_sum(src, seg, n)
kernel_name = 'mk_metaformer_d1_conv_nchw256_r4_6d8907'

def setup_inputs(seed: int=0):
    np.random.seed(seed)
    _w = jnp.asarray

    def _rec_inputs():
        import jax
        import jax.numpy as jnp
        _gk = jax.random.key(seed)
        x = -0.0002091 + 1 * jax.random.normal(jax.random.fold_in(_gk, 1), (32, 64, 56, 56), jnp.float32)
        return x
    x = _rec_inputs()

    def _L0_conv_setup():
        import jax, jax.numpy as jnp
        import numpy as np
        N, C, H, W = (32, 64, 56, 56)
        EPS = 1e-05

        def bin_act(x):
            return jnp.sign(x)

        def bin_weight(w):
            scale = jnp.mean(jnp.abs(w), axis=(1, 2, 3), keepdims=True)
            return jnp.sign(w) * scale

        def conv(x, w, stride, pad):
            return jax.lax.conv_general_dilated(x, w, (stride, stride), [(pad, pad), (pad, pad)], dimension_numbers=('NCHW', 'OIHW', 'NCHW'))

        def bn(x, gamma, beta, mean, var):
            c = lambda v: v[None, :, None, None]
            inv = gamma * jax.lax.rsqrt(var + EPS)
            return x * c(inv) + c(beta - mean * inv)

        def rprelu(x, move, slope, bias):
            c = lambda v: v[None, :, None, None]
            y = x + c(move)
            y = jnp.where(y > 0, y, c(slope) * y)
            return y + c(bias)
        key = jax.random.key(seed)
        ks = jax.random.split(key, 20)
        f = jnp.float32
        d = {}
        d['x'] = jax.random.normal(ks[0], (N, C, H, W), f)
        d['move1_bias'] = 0.01 * jax.random.normal(ks[1], (C,), f)
        d['w3'] = 0.1 * jax.random.normal(ks[2], (C, C, 3, 3), f)
        d['bn1_gamma'] = 1.0 + 0.1 * jax.random.normal(ks[3], (C,), f)
        d['bn1_beta'] = 0.1 * jax.random.normal(ks[4], (C,), f)
        d['bn1_mean'] = 0.1 * jax.random.normal(ks[5], (C,), f)
        d['bn1_var'] = jax.random.uniform(ks[6], (C,), f, 0.5, 1.5)
        d['prelu1_move'] = 0.01 * jax.random.normal(ks[7], (C,), f)
        d['prelu1_slope'] = 0.25 + 0.01 * jax.random.normal(ks[8], (C,), f)
        d['prelu1_bias'] = 0.01 * jax.random.normal(ks[9], (C,), f)
        d['move2_bias'] = 0.01 * jax.random.normal(ks[10], (C,), f)
        d['w_pw'] = 0.1 * jax.random.normal(ks[11], (C, C, 1, 1), f)
        d['bn2_gamma'] = 1.0 + 0.1 * jax.random.normal(ks[12], (C,), f)
        d['bn2_beta'] = 0.1 * jax.random.normal(ks[13], (C,), f)
        d['bn2_mean'] = 0.1 * jax.random.normal(ks[14], (C,), f)
        d['bn2_var'] = jax.random.uniform(ks[15], (C,), f, 0.5, 1.5)
        d['prelu2_move'] = 0.01 * jax.random.normal(ks[16], (C,), f)
        d['prelu2_slope'] = 0.25 + 0.01 * jax.random.normal(ks[17], (C,), f)
        d['prelu2_bias'] = 0.01 * jax.random.normal(ks[18], (C,), f)
        return d
    _L0_conv_all = _L0_conv_setup()
    _L0_conv_in = {k: v for k, v in _L0_conv_all.items() if k in ('move1_bias', 'w3', 'bn1_gamma', 'bn1_beta', 'bn1_mean', 'bn1_var', 'prelu1_move', 'prelu1_slope', 'prelu1_bias', 'move2_bias', 'w_pw', 'bn2_gamma', 'bn2_beta', 'bn2_mean', 'bn2_var', 'prelu2_move', 'prelu2_slope', 'prelu2_bias')}
    del _L0_conv_all

    def _L0_ffn_setup():
        import math
        import jax, jax.numpy as jnp
        import numpy as np
        CAPACITY_FACTOR = 1.25
        key = jax.random.key(seed)
        ks = jax.random.split(key, 5)
        B, L, D, F, E = (8, 2048, 64, 256, 8)
        h = jax.random.normal(ks[0], (B, L, D), dtype=jnp.float32)
        gate_w = jax.random.normal(ks[1], (D, E), dtype=jnp.float32) * 0.02
        gate_b = jnp.zeros((E,), dtype=jnp.float32)
        w1 = jax.random.normal(ks[2], (E, D, F), dtype=jnp.float32) * (1.0 / math.sqrt(D))
        b1 = jnp.zeros((E, F), dtype=jnp.float32)
        w2 = jax.random.normal(ks[3], (E, F, D), dtype=jnp.float32) * (1.0 / math.sqrt(F))
        b2 = jnp.zeros((E, D), dtype=jnp.float32)
        return {'h': h, 'gate_w': gate_w, 'gate_b': gate_b, 'w1': w1, 'b1': b1, 'w2': w2, 'b2': b2}
    _L0_ffn_all = _L0_ffn_setup()
    _L0_ffn_in = {k: v for k, v in _L0_ffn_all.items() if k in ('gate_w', 'gate_b', 'w1', 'b1', 'w2', 'b2')}
    del _L0_ffn_all
    return {'x': x, 'L0_conv_move1_bias': _L0_conv_in['move1_bias'], 'L0_conv_w3': _L0_conv_in['w3'], 'L0_conv_bn1_gamma': _L0_conv_in['bn1_gamma'], 'L0_conv_bn1_beta': _L0_conv_in['bn1_beta'], 'L0_conv_bn1_mean': _L0_conv_in['bn1_mean'], 'L0_conv_bn1_var': _L0_conv_in['bn1_var'], 'L0_conv_prelu1_move': _L0_conv_in['prelu1_move'], 'L0_conv_prelu1_slope': _L0_conv_in['prelu1_slope'], 'L0_conv_prelu1_bias': _L0_conv_in['prelu1_bias'], 'L0_conv_move2_bias': _L0_conv_in['move2_bias'], 'L0_conv_w_pw': _L0_conv_in['w_pw'], 'L0_conv_bn2_gamma': _L0_conv_in['bn2_gamma'], 'L0_conv_bn2_beta': _L0_conv_in['bn2_beta'], 'L0_conv_bn2_mean': _L0_conv_in['bn2_mean'], 'L0_conv_bn2_var': _L0_conv_in['bn2_var'], 'L0_conv_prelu2_move': _L0_conv_in['prelu2_move'], 'L0_conv_prelu2_slope': _L0_conv_in['prelu2_slope'], 'L0_conv_prelu2_bias': _L0_conv_in['prelu2_bias'], 'L0_ffn_gate_w': _L0_ffn_in['gate_w'], 'L0_ffn_gate_b': _L0_ffn_in['gate_b'], 'L0_ffn_w1': _L0_ffn_in['w1'], 'L0_ffn_b1': _L0_ffn_in['b1'], 'L0_ffn_w2': _L0_ffn_in['w2'], 'L0_ffn_b2': _L0_ffn_in['b2']}

def reference(x, L0_conv_move1_bias, L0_conv_w3, L0_conv_bn1_gamma, L0_conv_bn1_beta, L0_conv_bn1_mean, L0_conv_bn1_var, L0_conv_prelu1_move, L0_conv_prelu1_slope, L0_conv_prelu1_bias, L0_conv_move2_bias, L0_conv_w_pw, L0_conv_bn2_gamma, L0_conv_bn2_beta, L0_conv_bn2_mean, L0_conv_bn2_var, L0_conv_prelu2_move, L0_conv_prelu2_slope, L0_conv_prelu2_bias, L0_ffn_gate_w, L0_ffn_gate_b, L0_ffn_w1, L0_ffn_b1, L0_ffn_w2, L0_ffn_b2):
    import jax
    import jax.numpy as jnp

    def _L0_conv_ref(x, move1_bias, w3, bn1_gamma, bn1_beta, bn1_mean, bn1_var, prelu1_move, prelu1_slope, prelu1_bias, move2_bias, w_pw, bn2_gamma, bn2_beta, bn2_mean, bn2_var, prelu2_move, prelu2_slope, prelu2_bias):
        import jax, jax.numpy as jnp
        import numpy as np
        N, C, H, W = (32, 64, 56, 56)
        EPS = 1e-05

        def bin_act(x):
            return jnp.sign(x)

        def bin_weight(w):
            scale = jnp.mean(jnp.abs(w), axis=(1, 2, 3), keepdims=True)
            return jnp.sign(w) * scale

        def conv(x, w, stride, pad):
            return jax.lax.conv_general_dilated(x, w, (stride, stride), [(pad, pad), (pad, pad)], dimension_numbers=('NCHW', 'OIHW', 'NCHW'))

        def bn(x, gamma, beta, mean, var):
            c = lambda v: v[None, :, None, None]
            inv = gamma * jax.lax.rsqrt(var + EPS)
            return x * c(inv) + c(beta - mean * inv)

        def rprelu(x, move, slope, bias):
            c = lambda v: v[None, :, None, None]
            y = x + c(move)
            y = jnp.where(y > 0, y, c(slope) * y)
            return y + c(bias)
        out1 = x + move1_bias[None, :, None, None]
        out1 = conv(bin_act(out1), bin_weight(w3), 1, 1)
        out1 = bn(out1, bn1_gamma, bn1_beta, bn1_mean, bn1_var)
        out1 = x + out1
        out1 = rprelu(out1, prelu1_move, prelu1_slope, prelu1_bias)
        out2 = out1 + move2_bias[None, :, None, None]
        out2 = conv(bin_act(out2), bin_weight(w_pw), 1, 0)
        out2 = bn(out2, bn2_gamma, bn2_beta, bn2_mean, bn2_var)
        out2 = out2 + out1
        out2 = rprelu(out2, prelu2_move, prelu2_slope, prelu2_bias)
        return out2

    def _L0_ffn_ref(h, gate_w, gate_b, w1, b1, w2, b2):
        import math
        import jax, jax.numpy as jnp
        import numpy as np
        CAPACITY_FACTOR = 1.25
        B, L, D = h.shape
        E = gate_w.shape[1]
        T = B * L
        C = max(1, math.ceil(CAPACITY_FACTOR * T / E))
        x = h.reshape(T, D)
        logits = x @ gate_w + gate_b
        probs = jax.nn.softmax(logits, axis=-1)
        idx = jnp.argmax(probs, axis=-1)
        prb = jnp.take_along_axis(probs, idx[:, None], axis=1)[:, 0]
        one_hot = jax.nn.one_hot(idx, E, dtype=jnp.float32)
        pos = (jnp.cumsum(one_hot, axis=0) * one_hot).sum(-1).astype(jnp.int32) - 1
        kept = pos < C
        pos_safe = jnp.where(kept, pos, C)
        buf = jnp.zeros((E, C, D), dtype=h.dtype).at[idx, pos_safe].set(x, mode='drop')
        hmid = jax.nn.relu(jnp.einsum('ecd,edf->ecf', buf, w1) + b1[:, None, :])
        ybuf = jnp.einsum('ecf,efd->ecd', hmid, w2) + b2[:, None, :]
        pos_g = jnp.minimum(pos, C - 1)
        y_tok = ybuf[idx, pos_g] * (prb * kept)[:, None]
        y = y_tok.reshape(B, L, D)
        y = jnp.nan_to_num(y, nan=0.0, posinf=10000.0, neginf=-10000.0)
        return y

    def _gn(v, G=32, eps=1e-05):
        B_, C_, H_, W_ = v.shape
        g = v.reshape(B_, G, C_ // G, H_, W_)
        m = jnp.mean(g, axis=(2, 3, 4), keepdims=True)
        s = jnp.var(g, axis=(2, 3, 4), keepdims=True)
        return ((g - m) / jnp.sqrt(s + eps)).reshape(v.shape)

    def _ln_c(v, eps=1e-06):
        m = jnp.mean(v, axis=1, keepdims=True)
        s = jnp.var(v, axis=1, keepdims=True)
        return (v - m) / jnp.sqrt(s + eps)

    def _ln_t(v, eps=1e-05):
        m = jnp.mean(v, axis=-1, keepdims=True)
        s = jnp.var(v, axis=-1, keepdims=True)
        return (v - m) / jnp.sqrt(s + eps)

    def _to_tokens(v):
        B_, C_, H_, W_ = v.shape
        return v.reshape(B_, C_, H_ * W_).transpose(0, 2, 1)

    def _from_tokens(t, like):
        B_, C_, H_, W_ = like.shape
        return t.transpose(0, 2, 1).reshape(B_, C_, H_, W_)
    x = x + _L0_conv_ref(_ln_c(x), L0_conv_move1_bias, L0_conv_w3, L0_conv_bn1_gamma, L0_conv_bn1_beta, L0_conv_bn1_mean, L0_conv_bn1_var, L0_conv_prelu1_move, L0_conv_prelu1_slope, L0_conv_prelu1_bias, L0_conv_move2_bias, L0_conv_w_pw, L0_conv_bn2_gamma, L0_conv_bn2_beta, L0_conv_bn2_mean, L0_conv_bn2_var, L0_conv_prelu2_move, L0_conv_prelu2_slope, L0_conv_prelu2_bias)
    t = _to_tokens(x)
    t = t + _L0_ffn_ref(_ln_t(t), L0_ffn_gate_w, L0_ffn_gate_b, L0_ffn_w1, L0_ffn_b1, L0_ffn_w2, L0_ffn_b2)
    x = _from_tokens(t, x)
    return x

_drawn_inputs = setup_inputs


def setup_inputs(seed=0):
    import zlib

    import numpy as np

    out = dict(_drawn_inputs(seed))
    spreads = {'L0_ffn_gate_b': (0.0, 0.317), 'L0_ffn_b1': (0.0, 2.0), 'L0_ffn_b2': (0.0, 2.0)}
    factors = {'L0_conv_prelu1_move': 3.364,
     'L0_conv_prelu1_slope': 8.0,
     'L0_conv_prelu2_move': 8.0,
     'L0_conv_prelu2_slope': 8.0,
     'L0_conv_prelu2_bias': 39.21,
     'L0_conv_prelu1_bias': 6.01,
     'L0_conv_move2_bias': 5.892,
     'L0_conv_bn2_gamma': 4.224,
     'L0_ffn_gate_w': 2.8,
     'L0_ffn_w1': 4.812,
     'L0_ffn_w2': 3.33}
    for name, (base, spread) in spreads.items():
        noise = np.random.default_rng([zlib.crc32(name.encode()), seed]).standard_normal(out[name].shape)
        drawn = base * np.exp(spread * noise) if base else spread * noise
        out[name] = jnp.asarray(drawn.astype(out[name].dtype))
    for name, factor in factors.items():
        out[name] = (out[name] * factor).astype(out[name].dtype)
    return out
```

```python
import concourse.bass as bass
from concourse import mybir
from contextlib import ExitStack


def metaformer_kernel(nc, x, move1, w3, g1, be1, mu1, va1, pm1, ps1, pb1, move2, w_pw,
                      g2, be2, mu2, va2, pm2, ps2, pb2, gate_w, gate_b, w1, b1, w2, b2, out):
    fp32, bf16 = mybir.dt.float32, mybir.dt.bfloat16
    i32, u32 = mybir.dt.int32, mybir.dt.uint32
    ALU, ACT, AX = mybir.AluOpType, mybir.ActivationFunctionType, mybir.AxisListType
    ds = bass.ds

    IMAGES, C, H, W = x.shape
    E, _, F = w1.shape
    HW = H * W
    PAIRS = IMAGES // 2
    P = 2 * C
    TOKENS = IMAGES * HW
    CAPACITY = -(-5 * TOKENS // (4 * E))
    CHUNK_ROWS = 8
    NCH = H // CHUNK_ROWS
    CW = CHUNK_ROWS * W
    TILES = -(-HW // P)
    LAST = HW - (TILES - 1) * P
    SLOTS = 2 * TILES
    GROUP = 4
    NG = -(-TILES // GROUP)
    HP, WP = H + 2, W + 2
    TAPS = 9
    XBUF, ZBUF = 4, 3

    MEAN, RSTD, GATE, TOKEN = C, C + 1, C + 2, C + 3
    ROW = C + 4
    SUPER = 512
    SUB = SUPER // P
    REGION = TOKENS + SUPER
    IDLE = E * REGION
    NSUP = (TOKENS + E * (SUPER - 1)) // SUPER
    HC = F // P
    RING = 8
    EPS_C, EPS_T, EPS_BN = 1e-6, 1e-5, 1e-5
    LIMIT = 10000.0

    last_chunk = [min(((min((g + 1) * GROUP * P, HW)) - 1) // CW, NCH - 1) for g in range(NG)]
    group_tiles = [list(range(g * GROUP, min((g + 1) * GROUP, TILES))) for g in range(NG)]

    rows = nc.dram_tensor("rows_by_expert", (IDLE + SUPER, ROW), fp32).ap()
    done = nc.dram_tensor("rows_by_token", (TOKENS, C), fp32).ap()

    x_v = x.rearrange("(n i) c h w -> n (i c) (h w)", i=2)
    out_v = out.rearrange("(n i) c h w -> n (i c) (h w)", i=2)
    PJ = 28
    PP = HW // PJ
    NG3 = PJ // GROUP
    done_v = done.rearrange("(n p j i) c -> n p (j i c)", i=2, p=PP, j=PJ)

    ctx = ExitStack()
    with ctx:
        def sb(name, shape, dt=fp32):
            return ctx.enter_context(nc.sbuf_tensor(name, shape, dt))

        def sem(name):
            return ctx.enter_context(nc.semaphore(name))

        taken = {}

        def part_of(t, p, *shape):
            n = 1
            for d in shape:
                n *= d
            at = taken.get(t.name, 0)
            taken[t.name] = at + n
            names = "abc"[:len(shape)]
            dims = {k: d for k, d in zip(names, shape)}
            return t[0:p, at:at + n].rearrange(f"p ({' '.join(names)}) -> p {' '.join(names)}", **dims)
        X = sb("X", [P, XBUF * HW])
        Z = sb("Z", [P, ZBUF * HW])
        S1 = sb("S1", [P, 2, HP, WP], bf16)
        X2 = sb("X2", [P, TILES * P])
        ROWS = sb("ROWS", [P, 2, SLOTS, ROW])
        SQ = sb("SQ", [P, 2, CW])
        N1 = sb("N1", [P, 2, CW])
        N2 = sb("N2", [P, 2, CW])
        S2 = sb("S2", [P, 2, CW], bf16)
        VAR1 = sb("VAR1", [2 * NCH, CW])
        SD1 = sb("SD1", [2 * NCH, CW])
        RA1 = sb("RA1", [2 * NCH, CW])
        RB1 = sb("RB1", [2 * NCH, CW])
        RSTD1 = sb("RSTD1", [2 * NCH, CW])
        STATS = sb("STATS", [P, SLOTS, 6])
        msum, mdif, m2, d2, var2, sd2, r0, ra, rb = (
            sb(n, [P, SLOTS]) for n in ("msum", "mdif", "m2", "d2", "var2", "sd2", "r0", "ra", "rb"))
        mx, imin, ssum, prob, rowid, posn = (
            sb(n, [P, SLOTS]) for n in ("mx", "imin", "ssum", "prob", "rowid", "posn"))
        logit = sb("logit", [P, SLOTS, E])
        shifted = sb("shifted", [P, SLOTS, E])
        expo = sb("expo", [P, SLOTS, E])
        cand = sb("cand", [P, SLOTS, E])
        rowsel = sb("rowsel", [P, SLOTS, E])
        onehot = sb("onehot", [P, SLOTS, E], bf16)
        tile_tot = sb("tile_tot", [SLOTS, E], bf16)
        tile_off = sb("tile_off", [SLOTS, SLOTS, E], bf16)
        idx = sb("idx", [P, 2, SLOTS], u32)
        base = sb("base", [P, E])
        tokf = sb("tokf", [P, SLOTS])

        ident = sb("ident", [P, P])
        center = sb("center", [P, P])
        pick_var = sb("pick_var", [P, NCH, 2 * NCH])
        pick_bc = sb("pick_bc", [2 * NCH, NCH, P])
        upper = sb("upper", [P, P], bf16)
        ones = sb("ones", [P, P], bf16)
        earlier = sb("earlier", [SLOTS, SLOTS], bf16)
        iota8 = sb("iota8", [P, E])
        region0 = sb("region0", [P, E])
        gw2 = sb("gw2", [P, E])
        gate = sb("gate", [P, 2 * E])
        gb = sb("gb", [P, E])
        WB = sb("WB", [P, TAPS + 1, P], bf16)
        W3 = part_of(X2, P, C * TAPS)
        ABSW = part_of(X2, P, C * TAPS)
        SW = part_of(X2, P, TAPS + 1, P)
        WPW = sb("WPW", [P, C])
        ABSP = sb("ABSP", [P, C])
        PARAMS = ("va1", "va2", "g1", "g2", "be1", "be2", "mu1", "mu2",
                  "pm1", "pm2", "pb1", "pb2", "ps1", "ps2", "move1", "move2")
        prow = sb("prow", [len(PARAMS), P])
        par = sb("par", [P, len(PARAMS)])
        cst = sb("cst", [P, 32])

        RT = part_of(X, P, RING, SUB, ROW)
        XN = sb("XN", [P, 2, SUB, C])
        XT = sb("XT", [C, 2, SUPER])
        HB = part_of(X, P, 2, HC, SUPER)
        W1T = part_of(X, C, RING, F)
        W2T = part_of(X, P, RING, HC, C)
        B1T = sb("B1T", [P, RING, HC])
        B2T = sb("B2T", [P, RING, C])
        Y1 = sb("Y1", [P, SUB, C])
        Y2 = sb("Y2", [P, SUB, C])
        SGN = sb("SGN", [P, SUB, C])
        Y3 = sb("Y3", [P, SUB, C])
        FINITE = sb("FINITE", [P, SUB, C], i32)
        RES = part_of(X, P, RING, SUB, C)
        PAD = sb("PAD", [P, SUB, ROW])
        kio = sb("kio", [1, NSUP])
        tb = sb("tb", [1, 2, NSUP])
        tbe = sb("tbe", [1, 2, NSUP])
        tbi = sb("tbi", [1, 2, NSUP], i32)
        ind = sb("ind", [1, NSUP])
        ends = sb("ends", [1, E])
        endi = sb("endi", [1, E], i32)
        ntf = sb("ntf", [1, E])
        nti = sb("nti", [1, E], i32)
        ntp = sb("ntp", [1, E])
        ntd = sb("ntd", [1, E])

        bank = [ctx.enter_context(nc.psum_tensor(f"bank{n}", [P, 512], fp32)) for n in range(8)]
        MIX, VARP, CONV, PW, TRP, LOG, PRE = bank[0], bank[1], bank[2:4], bank[4], bank[5], bank[6], bank[7]
        TOT0, SUM0 = SLOTS * E, SLOTS * E + E

        s_param = sem("param_loaded")
        s_gate = sem("gate_loaded")
        s_w = sem("conv_weights_loaded")
        s_fill = sem("constants_filled")
        s_zero = sem("zeroed")
        s_absw = sem("abs_weights")
        s_sgn = sem("sign_weights")
        s_setp = sem("setup_products")
        s_setr = sem("setup_read")
        s_setstep = sem("setup_step")
        s_setsd = sem("setup_sqrt")
        s_const = sem("channel_constants")
        s_x = [sem("x_even_loaded"), sem("x_odd_loaded")]
        s_cen = sem("centered")
        s_xc = sem("centered_copied")
        s_sq = sem("squared")
        s_vp = sem("variance_partial")
        s_v1 = sem("variance_read")
        s_sd1 = sem("std_ready")
        s_nw = sem("newton_step")
        s_r1 = sem("rstd_ready")
        s_bc = sem("rstd_spread")
        s_xn = sem("normalized")
        s_s1 = sem("sign1_ready")
        s_cv = sem("conv_done")
        s_z1 = sem("sum1_ready")
        s_n1 = sem("negative1_ready")
        s_q1 = sem("prelu1_ready")
        s_s2 = sem("sign2_ready")
        s_pw = sem("pointwise_done")
        s_z2 = sem("sum2_ready")
        s_n2 = sem("negative2_ready")
        s_q2 = sem("prelu2_ready")
        s_x2 = sem("block_ready")
        s_tr = sem("rows_transposed")
        s_row = sem("rows_copied")
        s_st = sem("row_stats_ready")
        s_lg = sem("logits_done")
        s_lr = sem("logits_read")
        s_route = sem("route_step")
        s_rv = sem("row_variance")
        s_rs = sem("row_std")
        s_sh = sem("logits_shifted")
        s_ex = sem("exponentials")
        s_oh = sem("onehot_ready")
        s_tt = sem("tile_totals")
        s_of = sem("tile_offsets")
        s_pf = sem("prefix_ready")
        s_rr = sem("rows_routed")
        s_sc = [[sem(f"scattered_{'even' if k == 0 else 'odd'}_{g}") for g in range(NG)] for k in range(2)]
        s_pad = sem("padding_written")
        s_tab = sem("table_step")
        s_table = sem("table_ready")
        s_rt = [sem(f"super_rows_loaded_{k}") for k in range(RING)]
        s_we = [sem(f"expert_weights_loaded_{k}") for k in range(RING)]
        s_ln = sem("rows_normalized")
        s_pt = sem("super_transposed")
        s_xt = sem("super_columns_copied")
        s_h = sem("hidden_done")
        s_ha = sem("hidden_even_relu")
        s_hb = sem("hidden_odd_relu")
        s_y = sem("expert_output")
        s_g = sem("gating_step")
        s_res = sem("result_ready")
        s_back = [sem(f"results_scattered_{k}") for k in range(RING)]
        s_in3 = [sem("tokens_even_loaded"), sem("tokens_odd_loaded")]
        s_t3 = sem("images_transposed")
        s_c3 = sem("images_copied")
        s_past = sem("waits_passed")
        s_out = [sem("out_even_stored"), sem("out_odd_stored")]

        block = ctx.enter_context(nc.Block())

        FILLS = 22
        VAR_STEP = 3
        ROUTE_AT = (0, 3, 9, 14, 15, 21)
        NROUTE = ROUTE_AT[-1]
        GSTEPS = 6

        def wait(eng, s, count):
            if isinstance(count, int) and count <= 0:
                return
            eng.wait_ge(s, count)

        def wait_apart(eng, s, count):
            wait(eng, s, count)
            if not isinstance(count, int):
                eng.sem_inc(s_past, 1)

        def super_tiles(eng, first, end, one):
            passes = (end - first) // RING
            with eng.Fori(0, passes) as n:
                for u in range(RING):
                    one(n * RING + (first + u), (first + u) % RING)
            for k in range(first + passes * RING, end):
                one(k, k % RING)

        class Pair:
            def __init__(self, n, odd):
                self.n, self.odd = n, odd

            def x(self, c=0, width=HW):
                return ds((self.n % XBUF) * HW + c, width)

            def z(self, c=0, width=CW):
                return ds((self.n % ZBUF) * HW + c, width)

        def software_pipeline(eng, stage):
            def run(i, odd):
                pick = lambda k: Pair(i + k, (odd + k) % 2)
                static = isinstance(i, int)
                ok = lambda k: not static or 0 <= i + k < PAIRS
                stage(*(pick(k) if ok(k) else None for k in (2, 1, 0, -1)))
            for i in (-2, -1, 0, 1):
                run(i, i % 2)
            with eng.Fori(0, PAIRS // 2 - 2) as n:
                run(n * 2 + 2, 0)
                run(n * 2 + 3, 1)
            for i in range(PAIRS - 2, PAIRS + 1):
                run(i, i % 2)

        def T3(odd):
            w = 2 * PJ * C
            return Z[0:PP, odd * w:odd * w + w]

        INV, BIAS, ABSM, S_, OMS = 0, 2, 4, 6, 8
        B1P, NB1P, CA, SG2, B2P, NB2P, CB, TS, TA, TBB = 10, 11, 12, 13, 14, 15, 16, 18, 20, 22
        col = lambda k, n=1: cst[:, k:k + n]
        prm = lambda name, n=1: par[:, PARAMS.index(name):PARAMS.index(name) + n]

        @block.gpsimd
        def _(pool):
            n = [0]

            def step(ins):
                n[0] += 1
                ins.then_inc(s_fill, 1)

            def fence():
                pool.wait_ge(s_fill, n[0])
            for t, v in ((ident, 0.0), (pick_var, 0.0), (pick_bc, 0.0), (upper, 1.0), (ones, 1.0),
                         (earlier, 1.0), (PAD, 0.0), (gate, 0.0)):
                step(pool.memset(t[:], v))
            step(pool.memset(center[:, :], 0.0))
            fence()
            for h in range(2):
                step(pool.memset(center[h * C:h * C + C, h * C:h * C + C], -1.0 / C))
            fence()
            step(pool.affine_select(out=ident[:], in_=ident[:], compare_op=ALU.not_equal, fill=1.0,
                                    base=0, pattern=[[-1, P]], channel_multiplier=1))
            step(pool.affine_select(out=center[:], in_=center[:], compare_op=ALU.not_equal, fill=1.0 - 1.0 / C,
                                    base=0, pattern=[[-1, P]], channel_multiplier=1))
            step(pool.affine_select(out=upper[:], in_=upper[:], compare_op=ALU.is_ge, fill=0.0,
                                    base=0, pattern=[[1, P]], channel_multiplier=-1))
            step(pool.affine_select(out=earlier[:], in_=earlier[:], compare_op=ALU.is_gt, fill=0.0,
                                    base=0, pattern=[[1, SLOTS]], channel_multiplier=-1))
            for h in range(2):
                part = pick_var[h * C:h * C + C]
                fence()
                step(pool.affine_select(out=part, in_=part, compare_op=ALU.not_equal, fill=1.0 / C, base=h,
                                        pattern=[[2, NCH], [-1, 2 * NCH]], channel_multiplier=0))
            fence()
            v = pick_bc[:].rearrange("r c (h m) -> r c h m", h=2)
            step(pool.affine_select(out=v, in_=v, compare_op=ALU.not_equal, fill=1.0, base=0,
                                    pattern=[[-2, NCH], [-1, 2], [0, C]], channel_multiplier=1))
            step(pool.iota(iota8[:], pattern=[[1, E]], base=-E, channel_multiplier=0,
                           allow_small_or_imprecise_dtypes=True))
            step(pool.iota(tokf[:].rearrange("p (h k) -> p h k", h=2), pattern=[[1, 2], [2 * P, TILES]], base=0,
                           channel_multiplier=2, allow_small_or_imprecise_dtypes=True))
            step(pool.iota(kio[:], pattern=[[1, NSUP]], base=0, channel_multiplier=0,
                           allow_small_or_imprecise_dtypes=True))
            fence()
            step(pool.iota(PAD[:, :, TOKEN].bitcast(i32), pattern=[[0, SUB]], base=TOKENS, channel_multiplier=0))
            assert n[0] == FILLS

            def scatter_pair(p):
                wait_apart(pool, s_rr, p.n + 1)
                for g in range(NG):
                    for k in group_tiles[g]:
                        live = P if k < TILES - 1 else LAST
                        for h in range(2):
                            s = h * TILES + k
                            pool.indirect_dma_start(
                                rows, bass.IndirectOffsetOnAxis(ap=idx[0:live, p.odd, s:s + 1], axis=0),
                                ROWS[0:live, p.odd, s, :], None).then_inc(s_sc[p.odd][g], 16)
            with pool.Fori(0, PAIRS // 2) as n_i:
                i = n_i * 2
                scatter_pair(Pair(i, 0))
                scatter_pair(Pair(i + 1, 1))

            def scatter_super(k, u):
                wait_apart(pool, s_res, k + 1)
                for j in range(SUB):
                    pool.indirect_dma_start(
                        done, bass.IndirectOffsetOnAxis(ap=RT[:, u, j, TOKEN:TOKEN + 1].bitcast(u32), axis=0),
                        RES[:, u, j, :], None, bounds_check=TOKENS - 1, oob_is_err=False,
                    ).then_inc(s_back[u], 16)
            super_tiles(pool, 0, NSUP, scatter_super)

        @block.sync
        def _(sp):
            for k, ap in enumerate((va1, va2, g1, g2, be1, be2, mu1, mu2)):
                sp.dma_start(prow[k:k + 1, 0:C], ap.rearrange("(a c) -> a c", a=1)).then_inc(s_param, 16)
            for h in range(2):
                sp.dma_start(W3[h * C:h * C + C, :], w3.rearrange("o i a b -> o (i a b)")).then_inc(s_w, 16)
                sp.dma_start(WPW[h * C:h * C + C, :], w_pw.rearrange("o i a b -> o (i a b)")).then_inc(s_w, 16)

            def load(p):
                sp.dma_start(X[:, p.x()], x_v[ds(p.n, 1)].rearrange("a p m -> (a p) m")).then_inc(s_x[p.odd], 16)
            load(Pair(0, 0))
            load(Pair(1, 1))
            for k in (2, 3):
                sp.wait_ge(s_x[k % 2], 16)
                load(Pair(k, k % 2))
            with sp.Fori(0, (PAIRS - XBUF) // 2) as n_i:
                i = n_i * 2 + XBUF
                for k in range(2):
                    wait(sp, s_x2, (i + k - XBUF + 1) * NCH)
                    load(Pair(i + k, k))
            sp.wait_ge(s_fill, FILLS)
            pad_rows = lambda at: rows[ds(at, SUPER), :].rearrange("(p j) c -> p j c", j=SUB)
            sp.dma_start(pad_rows(IDLE), PAD[:]).then_inc(s_pad, 16)
            sp.wait_ge(s_table, 1)
            for e in range(E):
                end = sp.value_load(endi[0:1, e:e + 1], min_val=e * REGION, max_val=e * REGION + TOKENS)
                sp.dma_start(pad_rows(end), PAD[:]).then_inc(s_pad, 16)
            sp.wait_ge(s_pad, 16 * (E + 1))
            for k in range(2):
                for g in range(NG):
                    sp.wait_ge(s_sc[k][g], 16 * 2 * len(group_tiles[g]) * (PAIRS // 2))

            def super_tile(k, u, first):
                at = sp.value_load(tbi[0:1, 0, ds(k, 1)], min_val=0, max_val=IDLE)
                e = sp.value_load(tbi[0:1, 1, ds(k, 1)], min_val=0, max_val=E - 1)
                if not first:
                    wait(sp, s_back[u], (k - u) * (16 * SUB // RING))
                sp.dma_start(RT[:, u], pad_rows(at)).then_inc(s_rt[u], 16)
                sp.dma_start(W1T[:, u, :], w1[ds(e, 1)].rearrange("a c f -> (a c) f")).then_inc(s_we[u], 16)
                sp.dma_start(W2T[:, u], w2[ds(e, 1)].rearrange("a (p c) d -> (a p) c d", c=HC)).then_inc(s_we[u], 16)
                sp.dma_start(B1T[:, u, :], b1[ds(e, 1)].rearrange("a (p c) -> (a p) c", c=HC)).then_inc(s_we[u], 16)
                sp.dma_start(B2T[:, u, :], b2[ds(e, 1), :].to_broadcast([P, C])).then_inc(s_we[u], 16)
            for u in range(RING):
                super_tile(u, u, True)
            super_tiles(sp, RING, NSUP, lambda k, u: super_tile(k, u, False))

            for u in range(RING):
                sp.wait_ge(s_back[u], 16 * SUB * len(range(u, NSUP, RING)))

            def load3(q, odd):
                sp.dma_start(T3(odd), done_v[ds(q, 1)].rearrange("a p m -> (a p) m")).then_inc(s_in3[odd], 16)

            def store3(q, odd):
                wait(sp, s_c3, NG3 * (q + 1))
                sp.dma_start(out_v[ds(q, 1)].rearrange("a p m -> (a p) m"),
                             X[:, odd * HW:odd * HW + HW]).then_inc(s_out[odd], 16)
            load3(0, 0)
            load3(1, 1)
            with sp.Fori(0, (PAIRS - 2) // 2) as n_q:
                q = n_q * 2
                for k in range(2):
                    store3(q + k, k)
                    load3(q + 2 + k, k)
            for k in range(2):
                store3(PAIRS - 2 + k, k)
            for k in range(2):
                sp.wait_ge(s_out[k], 16 * PAIRS // 2)

        @block.tensor
        def _(pe):
            mm = nc.tensor.matmul
            pe.wait_ge(s_fill, FILLS)
            pe.wait_ge(s_setstep, 1)
            nc.tensor.transpose(MIX[0:P, 0:len(PARAMS)], prow[:, :], ident[0:len(PARAMS), 0:len(PARAMS)]).then_inc(s_setp, 1)
            pe.wait_ge(s_gate, 48)
            mm(VARP[:, 0:E], center[:, :], gw2[:, :], start=True, stop=True).then_inc(s_setp, 1)
            pe.wait_ge(s_sgn, 4)
            for t0 in range(0, TAPS + 1, GROUP):
                bk = (CONV[0], CONV[1], PW)[t0 // GROUP]
                for t in range(t0, min(t0 + GROUP, TAPS + 1)):
                    last = nc.tensor.transpose(bk[:, (t - t0) * P:(t - t0 + 1) * P], SW[:, t, :], ident[:, :])
                last.then_inc(s_setp, 1)
            pe.wait_ge(s_const, 1)

            def one_pass(cen, nor, con, rou):
                for c in range(NCH + 2):
                    if rou and c == 3:
                        wait(pe, s_oh, rou.n + 1)
                        for e in range(E):
                            last = mm(PRE[0:SLOTS, TOT0 + e:TOT0 + e + 1], onehot[:, :, e], ones[:, 0:1],
                                      start=True, stop=True)
                        last.then_inc(s_tt, 1)
                    if rou and c == 4:
                        wait(pe, s_of, rou.n + 1)
                        mm(PRE[:, SUM0:SUM0 + E], ones[0:SLOTS, :], tile_tot[:, :], start=True, stop=True)
                        mm(PRE[:, 0:SLOTS * E], upper[:, :], onehot[:].rearrange("p s e -> p (s e)"),
                           start=True, stop=False)
                        mm(PRE[:, 0:SLOTS * E], ones[0:SLOTS, :], tile_off[:].rearrange("p s e -> p (s e)"),
                           start=False, stop=True).then_inc(s_pf, 1)
                    if cen and c < NCH:
                        if c == 0:
                            wait(pe, s_x[cen.odd], (cen.n - cen.odd) * 8 + 16)
                        wait(pe, s_xn, (cen.n - 1) * NCH + c)
                        mm(MIX[:, 0:CW], center[:, :], X[:, cen.x(c * CW, CW)], start=True, stop=True).then_inc(s_cen, 1)
                    if con and c < NCH:
                        wait(pe, s_s1, con.n * NCH + min(c + 2, NCH))
                        wait(pe, s_z1, con.n * NCH + max(c - 1, 0))
                        for t in range(TAPS):
                            dy, dx = t // 3, t % 3
                            last = mm(CONV[c % 2][:, 0:CW], WB[:, t, :],
                                      S1[:, con.odd, c * CHUNK_ROWS + dy:(c + 1) * CHUNK_ROWS + dy, dx:dx + W],
                                      start=t == 0, stop=t == TAPS - 1)
                        last.then_inc(s_cv, 1)
                    if nor and c < NCH:
                        if c == 0:
                            wait(pe, s_r1, nor.n + 1)
                        wait(pe, s_sq, (nor.n + 1) * NCH + c + 1 if cen else PAIRS * NCH)
                        if not cen:
                            wait(pe, s_xn, nor.n * NCH + c)
                        mm(MIX[:, 0:CW], pick_bc[:, c, :], RSTD1[:, :], start=True, stop=True).then_inc(s_bc, 1)
                    if con and 1 <= c <= NCH:
                        wait(pe, s_s2, con.n * NCH + c)
                        wait(pe, s_z2, con.n * NCH + c - 1)
                        mm(PW[:, 0:CW], WB[:, TAPS, :], S2[:, (c - 1) % 2, :], start=True, stop=True).then_inc(s_pw, 1)
                    if cen and c < NCH:
                        wait(pe, s_sq, cen.n * NCH + c + 1)
                        if c == 0:
                            wait(pe, s_v1, cen.n)
                        mm(VARP[0:2 * NCH, 0:CW], pick_var[:, c, :], SQ[:, c % 2, :],
                           start=c == 0, stop=c == NCH - 1).then_inc(s_vp, 1)
                    if con:
                        for g in range(NG):
                            if min(last_chunk[g] + 2, NCH + 1) != c:
                                continue
                            wait(pe, s_x2, con.n * NCH + last_chunk[g] + 1)
                            wait(pe, s_row, con.n * NG + g)
                            for k in group_tiles[g]:
                                last = nc.tensor.transpose(TRP[:, (k % GROUP) * P:(k % GROUP + 1) * P],
                                                           X2[:, k * P:(k + 1) * P], ident[:, :])
                            last.then_inc(s_tr, 1)
                            if g == 0:
                                wait(pe, s_lr, con.n)
                            for k in group_tiles[g]:
                                last = mm(LOG[:, k * 2 * E:(k + 1) * 2 * E], X2[:, k * P:(k + 1) * P], gate[:, :],
                                          start=True, stop=True)
                            last.then_inc(s_lg, 1)
            software_pipeline(pe, one_pass)

            PT, HH, YY = bank[0:2], (bank[2], bank[3]), bank[4:6]

            def super_pass(k, ring, t=True, l1=True, l2=True):
                if t:
                    b = (ring + 1) % 2
                    wait(pe, s_ln, k + 2)
                    wait_apart(pe, s_xt, k)
                    for j in range(SUB):
                        last = nc.tensor.transpose(PT[b][0:C, j * P:(j + 1) * P], XN[:, b, j, :], ident[:, :])
                    last.then_inc(s_pt, 1)
                if l1:
                    wait(pe, s_we[ring], (k - ring) * (64 // RING) + 64)
                    wait(pe, s_xt, k + 1)
                    for c in range(HC):
                        wait(pe, (s_ha, s_hb)[c], k)
                        mm(HH[c][:, :], W1T[:, ring, c::HC], XT[:, ring % 2, :], start=True, stop=True).then_inc(s_h, 1)
                if l2:
                    b = (ring - 1) % RING
                    wait(pe, s_ha, k)
                    wait(pe, s_hb, k)
                    wait(pe, s_g, (k - 2) * GSTEPS)
                    for j in range(SUB):
                        for c in range(HC):
                            last = mm(YY[b % 2][:, j * C:(j + 1) * C], HB[:, b % 2, c, j * P:(j + 1) * P],
                                      W2T[:, b, c, :], start=c == 0, stop=c == HC - 1)
                    last.then_inc(s_y, 1)
            super_pass(-1, -1 % RING, l1=False, l2=False)
            super_pass(0, 0, l2=False)
            super_pass(1, 1)
            super_pass(2, 2)
            super_tiles(pe, 3, NSUP - 1, super_pass)
            super_pass(NSUP - 1, (NSUP - 1) % RING, t=False)
            super_pass(NSUP, NSUP % RING, t=False, l1=False)

            def images(q, odd):
                wait(pe, s_in3[odd], (q - odd) * 8 + 16)
                for g in range(NG3):
                    wait(pe, s_c3, (q - 1) * NG3 + g + 1)
                    for j in range(GROUP):
                        t = (g * GROUP + j) * P
                        last = nc.tensor.transpose(bank[g][:, j * PP:(j + 1) * PP],
                                                   T3(odd)[:, t:t + P], ident[0:PP, 0:PP])
                    last.then_inc(s_t3, 1)
            images(0, 0)
            images(1, 1)
            with pe.Fori(0, (PAIRS - 2) // 2) as n_q:
                q = n_q * 2 + 2
                images(q, 0)
                images(q + 1, 1)

        @block.scalar
        def _(act):
            A = nc.scalar.activation
            for k, ap in enumerate((pm1, pm2, pb1, pb2, ps1, ps2, move1, move2)):
                act.dma_start(prow[8 + k:9 + k, 0:C], ap.rearrange("(a c) -> a c", a=1)).then_inc(s_param, 16)
            for h in range(2):
                act.dma_start(gw2[h * C:h * C + C, :], gate_w).then_inc(s_gate, 16)
            act.dma_start(gb[:, :], gate_b.rearrange("(a e) -> a e", a=1).to_broadcast([P, E])).then_inc(s_gate, 16)
            act.wait_ge(s_w, 64)
            A(ABSW[:, :], W3[:, :], ACT.Abs).then_inc(s_absw, 1)
            A(ABSP[:, :], WPW[:, :], ACT.Abs).then_inc(s_absw, 1)
            act.wait_ge(s_zero, 1)
            for h in range(2):
                b = slice(h * C, h * C + C)
                A(SW[b, 0:TAPS, b], W3[b, :].rearrange("o (i t) -> o t i", t=TAPS), ACT.Sign).then_inc(s_sgn, 1)
                A(SW[b, TAPS, b], WPW[b, :], ACT.Sign).then_inc(s_sgn, 1)
            act.wait_ge(s_setstep, VAR_STEP)
            A(col(TS, 2), col(TA, 2), ACT.Sqrt).then_inc(s_setsd, 1)
            act.wait_ge(s_const, 1)

            def one_pass(cen, nor, con, rou):
                for c in range(NCH + 2):
                    if cen and c < NCH:
                        wait(act, s_cen, cen.n * NCH + c + 1)
                        wait_apart(act, s_x2, (cen.n - ZBUF) * NCH + c + 1)
                        A(Z[:, cen.z(c * CW)], MIX[:, 0:CW], ACT.Copy).then_inc(s_xc, 1)
                        wait(act, s_vp, cen.n * NCH + c - 1)
                        A(SQ[:, c % 2, :], MIX[:, 0:CW], ACT.Square).then_inc(s_sq, 1)
                    if con and c < NCH:
                        wait_apart(act, s_z1, con.n * NCH + c + 1)
                        A(N1[:, c % 2, :], Z[:, con.z(c * CW)], ACT.Relu, bias=col(NB1P), scale=-1.0).then_inc(s_n1, 1)
                    if nor and c < NCH:
                        wait_apart(act, s_xn, nor.n * NCH + c + 1)
                        A(S1[:, nor.odd, 1 + c * CHUNK_ROWS:1 + (c + 1) * CHUNK_ROWS, 1:1 + W],
                          Z[:, nor.z(c * CW)].rearrange("p (r w) -> p r w", w=W), ACT.Sign,
                          bias=prm("move1")).then_inc(s_s1, 1)
                    if con and c < NCH:
                        wait_apart(act, s_q1, con.n * NCH + c + 1)
                        A(S2[:, c % 2, :], Z[:, con.z(c * CW)], ACT.Sign, bias=col(SG2)).then_inc(s_s2, 1)
                    if con and 1 <= c <= NCH:
                        wait_apart(act, s_z2, con.n * NCH + c)
                        A(N2[:, (c - 1) % 2, :], Z[:, con.z((c - 1) * CW)], ACT.Relu, bias=col(NB2P),
                          scale=-1.0).then_inc(s_n2, 1)
                    if con:
                        for g in range(NG):
                            if min(last_chunk[g] + 2, NCH + 1) != c:
                                continue
                            wait(act, s_tr, con.n * NG + g + 1)
                            n = len(group_tiles[g])
                            wait(act, s_sc[con.odd][g], (con.n - con.odd) * 16 * n)
                            dst = ROWS[:, con.odd].rearrange("p (h k) r -> p k h r", h=2)
                            A(dst[:, g * GROUP:g * GROUP + n, :, 0:C],
                              TRP[:, 0:n * P].rearrange("p (k h c) -> p k h c", h=2, c=C), ACT.Copy).then_inc(s_row, 1)
                    if rou and c == 0:
                        wait(act, s_rv, rou.n + 1)
                        A(sd2[:, :], var2[:, :], ACT.Sqrt).then_inc(s_rs, 1)
                    if rou and c == 1:
                        wait(act, s_sh, rou.n + 1)
                        A(expo[:], shifted[:], ACT.Exp).then_inc(s_ex, 1)
                    if cen and c == NCH - 1:
                        wait(act, s_v1, cen.n + 1)
                        A(SD1[:, :], VAR1[:, :], ACT.Sqrt).then_inc(s_sd1, 1)
            software_pipeline(act, one_pass)

            PT, HH = bank[0:2], (bank[2], bank[3])

            def super_pass(k, ring, t=True, h=True):
                if t:
                    b = (ring + 1) % 2
                    wait(act, s_pt, k + 2)
                    wait(act, s_h, HC * k)
                    A(XT[:, b, :], PT[b][0:C, :], ACT.Copy).then_inc(s_xt, 1)
                if h:
                    wait(act, s_h, HC * k + 1)
                    wait(act, s_y, k - 1)
                    A(HB[:, ring % 2, 0, :], HH[0][:, :], ACT.Relu, bias=B1T[:, ring, 0:1]).then_inc(s_ha, 1)
            super_pass(-1, -1 % RING, h=False)
            super_pass(0, 0)
            super_pass(1, 1)
            super_tiles(act, 2, NSUP - 1, super_pass)
            super_pass(NSUP - 1, (NSUP - 1) % RING, t=False)

            def copy_images(q, odd):
                wait(act, s_out[odd], (q - odd) * 8)
                for g in range(NG3):
                    wait(act, s_t3, q * NG3 + g + 1)
                    dst = X[:, odd * HW:odd * HW + HW].rearrange("p (t j) -> p j t", j=PJ)
                    A(dst[:, g * GROUP:(g + 1) * GROUP, :],
                      bank[g][:, 0:GROUP * PP].rearrange("p (j t) -> p j t", t=PP), ACT.Copy).then_inc(s_c3, 1)
            copy_images(0, 0)
            copy_images(1, 1)
            with act.Fori(0, PAIRS // 2 - 1) as n:
                copy_images(n * 2 + 2, 0)
                copy_images(n * 2 + 3, 1)

        @block.vector
        def _(dve):
            V = nc.vector
            n = [0]

            def step(ins):
                n[0] += 1
                ins.then_inc(s_setstep, 1)
                dve.wait_ge(s_setstep, n[0])
            V.memset(SW[:], 0.0).then_inc(s_zero, 1)
            V.memset(S1[:].bitcast(u32), 0)
            V.memset(X2[:, HW:], 0.0)
            V.memset(ROWS[:], 0.0)
            for e in range(E):
                V.memset(region0[:, e:e + 1], float(e * REGION - 1))
            dve.wait_ge(s_param, 16 * len(PARAMS))
            step(V.tensor_copy(prow[:, C:P], prow[:, 0:C]))
            dve.wait_ge(s_setp, 1)
            step(V.tensor_copy(par[:, :], MIX[:, 0:len(PARAMS)]))
            step(V.tensor_scalar(col(TA, 2), prm("va1", 2), EPS_BN, None, ALU.add))
            assert n[0] == VAR_STEP
            step(V.tensor_copy(base[:, :], region0[:, :]))
            dve.wait_ge(s_absw, 2)
            step(V.tensor_reduce(col(ABSM), ABSW[:, :], AX.X, ALU.add))
            step(V.tensor_reduce(col(ABSM + 1), ABSP[:, :], AX.X, ALU.add))
            step(V.tensor_scalar(col(ABSM), col(ABSM), 1.0 / (C * TAPS), None, ALU.mult))
            step(V.tensor_scalar(col(ABSM + 1), col(ABSM + 1), 1.0 / C, None, ALU.mult))
            dve.wait_ge(s_setsd, 1)
            step(V.reciprocal(col(TS, 2), col(TS, 2)))
            step(V.tensor_tensor(col(TBB, 2), col(TS, 2), col(TS, 2), ALU.mult))
            step(V.scalar_tensor_tensor(out=col(TBB, 2), in0=col(TBB, 2), scalar=-0.5, in1=col(TA, 2), op0=ALU.mult, op1=ALU.mult))
            step(V.scalar_tensor_tensor(out=col(TS, 2), in0=col(TBB, 2), scalar=1.5, in1=col(TS, 2), op0=ALU.add, op1=ALU.mult))
            step(V.tensor_tensor(col(INV, 2), col(TS, 2), prm("g1", 2), ALU.mult))
            step(V.tensor_tensor(col(S_, 2), col(INV, 2), col(ABSM, 2), ALU.mult))
            step(V.tensor_tensor(col(BIAS, 2), prm("mu1", 2), col(INV, 2), ALU.mult))
            step(V.tensor_tensor(col(BIAS, 2), prm("be1", 2), col(BIAS, 2), ALU.subtract))
            step(V.tensor_scalar(col(OMS, 2), prm("ps1", 2), -1.0, 1.0, ALU.mult, ALU.add))
            step(V.tensor_tensor(col(B1P), col(BIAS), prm("pm1"), ALU.add))
            step(V.tensor_scalar(col(NB1P), col(B1P), -1.0, None, ALU.mult))
            step(V.tensor_tensor(col(CA), col(B1P), prm("pb1"), ALU.add))
            step(V.tensor_tensor(col(SG2), col(CA), prm("move2"), ALU.add))
            step(V.tensor_tensor(col(B2P), col(BIAS + 1), col(CA), ALU.add))
            step(V.tensor_tensor(col(B2P), col(B2P), prm("pm2"), ALU.add))
            step(V.tensor_scalar(col(NB2P), col(B2P), -1.0, None, ALU.mult))
            step(V.tensor_tensor(col(CB), col(B2P), prm("pb2"), ALU.add))
            dve.wait_ge(s_setp, 5)
            dve.wait_ge(s_fill, FILLS)
            for h in range(2):
                step(V.tensor_copy(gate[h * C:h * C + C, h * E:h * E + E], VARP[h * C:h * C + C, 0:E]))
            for t0 in range(0, TAPS + 1, GROUP):
                t1 = min(t0 + GROUP, TAPS + 1)
                bk = (CONV[0], CONV[1], PW)[t0 // GROUP]
                step(V.tensor_copy(WB[:, t0:t1, :], bk[:, 0:(t1 - t0) * P].rearrange("p (t m) -> p t m", m=P)))
            V.memset(cst[:, 30:31], 0.0).then_inc(s_const, 1)

            over = lambda ap, m: ap.unsqueeze(1).to_broadcast([P, SLOTS, m])
            spread = lambda ap: ap.unsqueeze(2).to_broadcast([P, SLOTS, E])
            flat = lambda t: t[:].rearrange("p s e -> p (s e)")
            st = lambda k: STATS[:, :, k]

            def route(p, c):
                r = [ROUTE_AT[c]]

                def op(ins, s=None):
                    if s is not None:
                        ins.then_inc(s, 1)
                        return
                    r[0] += 1
                    ins.then_inc(s_route, 1)
                    wait(dve, s_route, p.n * NROUTE + r[0])
                if c == 0:
                    wait(dve, s_st, (p.n + 1) * NG)
                    V.tensor_tensor(msum[:], st(1), st(4), ALU.add)
                    V.tensor_tensor(mdif[:], st(1), st(4), ALU.subtract)
                    op(V.tensor_tensor(m2[:], st(2), st(5), ALU.add))
                    op(V.scalar_tensor_tensor(out=d2[:], in0=mdif[:], scalar=C / 4.0, in1=mdif[:], op0=ALU.mult, op1=ALU.mult))
                    V.tensor_scalar(ROWS[:, p.odd, :, MEAN], msum[:], 0.5, None, ALU.mult)
                    op(V.tensor_tensor(m2[:], m2[:], d2[:], ALU.add))
                    op(V.tensor_scalar(var2[:], m2[:], 1.0 / C, EPS_T, ALU.mult, ALU.add), s_rv)
                if c == 1:
                    wait(dve, s_rs, p.n + 1)
                    op(V.reciprocal(r0[:], sd2[:]))
                    op(V.tensor_tensor(ra[:], r0[:], r0[:], ALU.mult))
                    op(V.scalar_tensor_tensor(out=rb[:], in0=ra[:], scalar=-0.5, in1=var2[:], op0=ALU.mult, op1=ALU.mult))
                    rstd = ROWS[:, p.odd, :, RSTD]
                    op(V.scalar_tensor_tensor(out=rstd, in0=rb[:], scalar=1.5, in1=r0[:], op0=ALU.add, op1=ALU.mult))
                    wait(dve, s_lg, (p.n + 1) * NG)
                    for h in range(2):
                        sl = slice(h * TILES, (h + 1) * TILES)
                        ins = V.tensor_tensor(
                            logit[:, sl, :], LOG[:, 0:SLOTS * E].rearrange("p (k h e) -> p k h e", h=2, e=E)[:, :, h, :],
                            ROWS[:, p.odd, sl, RSTD:RSTD + 1].to_broadcast([P, TILES, E]), ALU.mult)
                    ins.then_inc(s_lr, 1)
                    wait(dve, s_lr, p.n + 1)
                    op(V.tensor_tensor(logit[:], logit[:], over(gb[:, :], E), ALU.add))
                    op(V.tensor_reduce(mx[:], logit[:], AX.X, ALU.max))
                    op(V.tensor_tensor(shifted[:], logit[:], spread(mx[:]), ALU.subtract), s_sh)
                if c == 2:
                    wait(dve, s_sh, p.n + 1)
                    op(V.scalar_tensor_tensor(out=cand[:], in0=shifted[:], scalar=0.0, in1=over(iota8[:, :], E),
                                              op0=ALU.is_ge, op1=ALU.mult))
                    op(V.tensor_reduce(imin[:], cand[:], AX.X, ALU.min))
                    op(V.tensor_tensor(onehot[:], over(iota8[:, :], E), spread(imin[:]), ALU.is_equal))
                    op(V.memset(onehot[LAST:P].rearrange("p (h k) e -> p h k e", h=2)[:, :, TILES - 1, :], 0.0), s_oh)
                    wait(dve, s_ex, p.n + 1)
                    op(V.tensor_reduce(ssum[:], expo[:], AX.X, ALU.add))
                    op(V.reciprocal(prob[:], ssum[:]))
                if c == 3:
                    wait(dve, s_tt, p.n + 1)
                    op(V.tensor_copy(tile_tot[:, :], PRE[0:SLOTS, TOT0:TOT0 + E]))
                    op(V.tensor_tensor(tile_off[:], earlier[:, :].unsqueeze(2).to_broadcast([SLOTS, SLOTS, E]),
                                       tile_tot[:, :].unsqueeze(1).to_broadcast([SLOTS, SLOTS, E]), ALU.mult), s_of)
                if c == 4:
                    wait(dve, s_pf, p.n + 1)
                    op(V.tensor_tensor(rowsel[:], PRE[:, 0:SLOTS * E].rearrange("p (s e) -> p s e", e=E),
                                       over(base[:, :], E), ALU.add))
                    op(V.tensor_tensor(base[:, :], base[:, :], PRE[:, SUM0:SUM0 + E], ALU.add))
                    op(V.tensor_tensor(rowsel[:], rowsel[:], onehot[:], ALU.mult))
                    op(V.tensor_reduce(rowid[:], rowsel[:], AX.X, ALU.add))
                    V.tensor_copy(idx[:, p.odd, :], rowid[:])
                    op(V.scalar_tensor_tensor(out=posn[:], in0=imin[:], scalar=-float(REGION), in1=rowid[:],
                                              op0=ALU.mult, op1=ALU.add))
                    V.tensor_copy(ROWS[:, p.odd, :, TOKEN].bitcast(u32), tokf[:])
                    op(V.scalar_tensor_tensor(out=ROWS[:, p.odd, :, GATE], in0=posn[:], scalar=float(E * REGION + CAPACITY),
                                              in1=prob[:], op0=ALU.is_lt, op1=ALU.mult))
                    V.tensor_scalar(tokf[:], tokf[:], float(2 * HW), None, ALU.add).then_inc(s_rr, 1)
                assert r[0] == ROUTE_AT[c + 1]

            def one_pass(cen, nor, con, rou):
                for c in range(NCH + 2):
                    if con and c < NCH:
                        wait(dve, s_cv, con.n * NCH + c + 1)
                        z = Z[:, con.z(c * CW)]
                        V.scalar_tensor_tensor(out=z, in0=CONV[c % 2][:, 0:CW], scalar=col(S_), in1=z,
                                               op0=ALU.mult, op1=ALU.add).then_inc(s_z1, 1)
                    if nor and c < NCH:
                        wait(dve, s_bc, nor.n * NCH + c + 1)
                        wait(dve, s_xc, nor.n * NCH + c + 1)
                        z = Z[:, nor.z(c * CW)]
                        V.tensor_tensor(z, z, MIX[:, 0:CW], ALU.mult).then_inc(s_xn, 1)
                    if con and c < NCH:
                        wait(dve, s_n1, con.n * NCH + c + 1)
                        z = Z[:, con.z(c * CW)]
                        V.scalar_tensor_tensor(out=z, in0=N1[:, c % 2, :], scalar=col(OMS), in1=z,
                                               op0=ALU.mult, op1=ALU.add).then_inc(s_q1, 1)
                    if con and 1 <= c <= NCH:
                        wait(dve, s_pw, con.n * NCH + c)
                        z = Z[:, con.z((c - 1) * CW)]
                        V.scalar_tensor_tensor(out=z, in0=PW[:, 0:CW], scalar=col(S_ + 1), in1=z,
                                               op0=ALU.mult, op1=ALU.add).then_inc(s_z2, 1)
                    if rou and c < 5:
                        route(rou, c)
                    if con and 1 <= c <= NCH:
                        wait(dve, s_n2, con.n * NCH + c)
                        z = Z[:, con.z((c - 1) * CW)]
                        V.scalar_tensor_tensor(out=z, in0=N2[:, (c - 1) % 2, :], scalar=col(OMS + 1), in1=z,
                                               op0=ALU.mult, op1=ALU.add).then_inc(s_q2, 1)
                    if con and 1 <= c <= NCH:
                        wait(dve, s_q2, con.n * NCH + c)
                        if c == 1:
                            wait(dve, s_lg, con.n * NG)
                        V.scalar_tensor_tensor(out=X2[:, (c - 1) * CW:c * CW], in0=Z[:, con.z((c - 1) * CW)],
                                               scalar=col(CB), in1=X[:, con.x((c - 1) * CW, CW)],
                                               op0=ALU.add, op1=ALU.add).then_inc(s_x2, 1)
                    if con:
                        for g in range(NG):
                            if min(last_chunk[g] + 2, NCH + 1) != c:
                                continue
                            wait(dve, s_row, con.n * NG + g + 1)
                            for k in group_tiles[g]:
                                for h in range(2):
                                    s = h * TILES + k
                                    last = V.bn_stats(STATS[:, s, :], ROWS[:, con.odd, s, 0:C])
                            last.then_inc(s_st, 1)
                    if cen and c == NCH - 1:
                        wait(dve, s_vp, (cen.n + 1) * NCH)
                        V.tensor_scalar(VAR1[:, :], VARP[0:2 * NCH, 0:CW], EPS_C, None, ALU.add).then_inc(s_v1, 1)
                        wait(dve, s_sd1, cen.n + 1)
                        V.reciprocal(RA1[:, :], SD1[:, :]).then_inc(s_nw, 1)
                        wait(dve, s_nw, cen.n * 3 + 1)
                        V.tensor_tensor(RB1[:, :], RA1[:, :], RA1[:, :], ALU.mult).then_inc(s_nw, 1)
                        wait(dve, s_nw, cen.n * 3 + 2)
                        V.scalar_tensor_tensor(out=RB1[:, :], in0=RB1[:, :], scalar=-0.5, in1=VAR1[:, :],
                                               op0=ALU.mult, op1=ALU.mult).then_inc(s_nw, 1)
                        wait(dve, s_nw, cen.n * 3 + 3)
                        wait(dve, s_bc, cen.n * NCH)
                        V.scalar_tensor_tensor(out=RSTD1[:, :], in0=RB1[:, :], scalar=1.5, in1=RA1[:, :],
                                               op0=ALU.add, op1=ALU.mult).then_inc(s_r1, 1)
            software_pipeline(dve, one_pass)

            m = [0]

            def tstep(ins):
                m[0] += 1
                ins.then_inc(s_tab, 1)
                dve.wait_ge(s_tab, m[0])
            dve.wait_ge(s_rr, PAIRS)
            tstep(V.tensor_scalar(ends[:, :], base[0:1, :], 1.0, None, ALU.add))
            tstep(V.tensor_copy(endi[:, :], ends[:, :]))
            tstep(V.tensor_tensor(ntf[:, :], base[0:1, :], region0[0:1, :], ALU.subtract))
            tstep(V.tensor_scalar(ntf[:, :], ntf[:, :], float(SUPER - 1), None, ALU.add))
            tstep(V.tensor_copy(nti[:, :], ntf[:, :]))
            tstep(V.tensor_scalar(nti[:, :], nti[:, :], SUPER.bit_length() - 1, None, ALU.arith_shift_right))
            tstep(V.tensor_copy(ntf[:, :], nti[:, :]))
            tstep(V.tensor_copy(ntp[:, :], ntf[:, :]))
            for e in range(1, E):
                tstep(V.tensor_tensor(ntp[:, e:e + 1], ntp[:, e:e + 1], ntp[:, e - 1:e], ALU.add))
            tstep(V.tensor_scalar(ntd[:, :], ntf[:, :], -float(SUPER), float(REGION), ALU.mult, ALU.add))
            tstep(V.tensor_scalar(tb[:, 0, :], kio[:, :], float(SUPER), None, ALU.mult))
            tstep(V.memset(tb[:, 1, :], 0.0))
            for e in range(E):
                tstep(V.tensor_scalar(ind[:, :], kio[:, :], ntp[:, e:e + 1], ntd[:, e:e + 1], ALU.is_ge, ALU.mult))
                tstep(V.tensor_tensor(tb[:, 0, :], tb[:, 0, :], ind[:, :], ALU.add))
                tstep(V.scalar_tensor_tensor(out=tb[:, 1, :], in0=kio[:, :], scalar=ntp[:, e:e + 1], in1=tb[:, 1, :],
                                             op0=ALU.is_ge, op1=ALU.add))
            tstep(V.tensor_scalar(tbe[:, 0, :], tb[:, 0, :], float(IDLE), None, ALU.min))
            tstep(V.tensor_scalar(tbe[:, 1, :], tb[:, 1, :], float(E - 1), None, ALU.min))
            V.tensor_copy(tbi[:], tbe[:]).then_inc(s_table, 1)

            HH, YY = (bank[2], bank[3]), bank[4:6]

            def super_pass(k, ring, ln=True, h=True, fin=True):
                if ln:
                    u, b = (ring + 2) % RING, ring % 2
                    wait(dve, s_rt[u], (k + 2 - u) * (16 // RING) + 16)
                    wait(dve, s_pt, k + 1)
                    for j in range(SUB):
                        last = V.tensor_scalar(XN[:, b, j, :], RT[:, u, j, 0:C], RT[:, u, j, MEAN:MEAN + 1],
                                               RT[:, u, j, RSTD:RSTD + 1], ALU.subtract, ALU.mult)
                    last.then_inc(s_ln, 1)
                if h:
                    wait(dve, s_h, HC * k + 2)
                    wait(dve, s_y, k - 1)
                    V.tensor_scalar(HB[:, ring % 2, 1, :], HH[1][:, :], B1T[:, ring, 1:2], 0.0,
                                    ALU.add, ALU.max).then_inc(s_hb, 1)
                if fin:
                    u = (ring - 1) % RING
                    g = [0]

                    def gstep(ins, wait=wait):
                        g[0] += 1
                        ins.then_inc(s_g, 1)
                        wait(dve, s_g, (k - 1) * GSTEPS + g[0])
                    wait(dve, s_y, k)
                    y = YY[u % 2][:, 0:SUB * C].rearrange("p (j c) -> p j c", c=C)
                    gstep(V.tensor_tensor(Y1[:], y, B2T[:, u, :].unsqueeze(1).to_broadcast([P, SUB, C]), ALU.add))
                    gstep(V.tensor_tensor(Y2[:], Y1[:], RT[:, u, :, GATE:GATE + 1].to_broadcast([P, SUB, C]), ALU.mult))
                    V.tensor_scalar(FINITE[:], Y2[:], 0.0, 0.0, ALU.mult, ALU.is_equal)
                    gstep(V.tensor_scalar(SGN[:], Y2[:], 0.0, None, ALU.is_gt))
                    gstep(V.scalar_tensor_tensor(out=SGN[:], in0=Y2[:], scalar=0.0, in1=SGN[:], op0=ALU.is_lt, op1=ALU.subtract))
                    gstep(V.tensor_scalar(Y3[:], SGN[:], -LIMIT, None, ALU.mult), wait_apart)
                    gstep(V.copy_predicated(Y3[:], FINITE[:], Y2[:]))
                    assert g[0] == GSTEPS
                    V.tensor_tensor(RES[:, u], Y3[:], RT[:, u, :, 0:C], ALU.add).then_inc(s_res, 1)
            super_pass(-2, -2 % RING, h=False, fin=False)
            super_pass(-1, -1 % RING, h=False, fin=False)
            super_pass(0, 0, fin=False)
            super_pass(1, 1)
            super_tiles(dve, 2, NSUP - 2, super_pass)
            super_pass(NSUP - 2, (NSUP - 2) % RING, ln=False)
            super_pass(NSUP - 1, (NSUP - 1) % RING, ln=False)
            super_pass(NSUP, NSUP % RING, ln=False, h=False)


_INS = ['x', 'L0_conv_move1_bias', 'L0_conv_w3', 'L0_conv_bn1_gamma', 'L0_conv_bn1_beta', 'L0_conv_bn1_mean',
        'L0_conv_bn1_var', 'L0_conv_prelu1_move', 'L0_conv_prelu1_slope', 'L0_conv_prelu1_bias', 'L0_conv_move2_bias',
        'L0_conv_w_pw', 'L0_conv_bn2_gamma', 'L0_conv_bn2_beta', 'L0_conv_bn2_mean', 'L0_conv_bn2_var',
        'L0_conv_prelu2_move', 'L0_conv_prelu2_slope', 'L0_conv_prelu2_bias', 'L0_ffn_gate_w', 'L0_ffn_gate_b',
        'L0_ffn_w1', 'L0_ffn_b1', 'L0_ffn_w2', 'L0_ffn_b2']


def kernel(**inputs):
    import numpy as _np
    import concourse.bacc as _bacc
    from concourse import mybir as _mybir
    from concourse.bass_utils import run_bass_kernel_spmd as _run

    nc = _bacc.Bacc("TRN2", target_bir_lowering=False, num_devices=1)
    arrays, args = {}, []
    for name in _INS:
        a = _np.ascontiguousarray(inputs[name])
        arrays[f"in_{name}_dram"] = a
        args.append(nc.dram_tensor(f"in_{name}_dram", a.shape, _mybir.dt.from_np(a.dtype), kind="ExternalInput").ap())
    shape = inputs['x'].shape
    args.append(nc.dram_tensor("out_0_dram", shape, _mybir.dt.float32, kind="ExternalOutput").ap())
    metaformer_kernel(nc, *args)
    r = _run(nc, [arrays], core_ids=[0])
    return r.results[0]["out_0_dram"]
```

```python
import concourse.bass as bass
from concourse import mybir
from contextlib import ExitStack


def metaformer_kernel(nc, x, move1, w3, g1, be1, mu1, va1, pm1, ps1, pb1, move2, w_pw,
                      g2, be2, mu2, va2, pm2, ps2, pb2, gate_w, gate_b, w1, b1, w2, b2, out):
    fp32, bf16 = mybir.dt.float32, mybir.dt.bfloat16
    i32, u32 = mybir.dt.int32, mybir.dt.uint32
    ALU, ACT, AX = mybir.AluOpType, mybir.ActivationFunctionType, mybir.AxisListType
    ds = bass.ds

    IMAGES, C, H, W = x.shape
    E, _, F = w1.shape
    HW = H * W
    PAIRS = IMAGES // 2
    P = 2 * C
    TOKENS = IMAGES * HW
    CAPACITY = -(-5 * TOKENS // (4 * E))
    CHUNK_ROWS = 8
    NCH = H // CHUNK_ROWS
    CW = CHUNK_ROWS * W
    TILES = -(-HW // P)
    LAST = HW - (TILES - 1) * P
    SLOTS = 2 * TILES
    GROUP = 4
    RGROUP = 3
    NG = -(-TILES // RGROUP)
    ME = 2 * E
    GW = P + 2 * E + 2
    HP, WP = H + 2, W + 2
    TAPS = 9
    XBUF, ZBUF = 4, 3

    MEAN, RSTD, GATE, TOKEN = C, C + 1, C + 2, C + 3
    ROW = C + 4
    SUPER = 512
    SUB = SUPER // P
    REGION = TOKENS + SUPER
    IDLE = E * REGION
    NSUP = (TOKENS + E * (SUPER - 1)) // SUPER
    HC = F // C
    DUO = SUPER // 2
    WCOLS = 2 * HC * P + HC + 1
    W2_AT, B1_AT, B2_AT = HC * P, 2 * HC * P, 2 * HC * P + HC
    RING = 8
    WRING = 4
    EPS_C, EPS_T, EPS_BN = 1e-6, 1e-5, 1e-5
    LIMIT = 10000.0

    last_chunk = [min(((min((g + 1) * RGROUP * P, HW)) - 1) // CW, NCH - 1) for g in range(NG)]
    group_tiles = [list(range(g * RGROUP, min((g + 1) * RGROUP, TILES))) for g in range(NG)]

    rows = nc.dram_tensor("rows_by_expert", (IDLE + SUPER, ROW), fp32).ap()
    done = nc.dram_tensor("rows_by_token", (TOKENS, C), fp32).ap()

    x_v = x.rearrange("(n i) c h w -> n (i c) (h w)", i=2)
    out_v = out.rearrange("(n i) c h w -> n (i c) (h w)", i=2)
    PJ = 28
    PP = HW // PJ
    NG3 = PJ // GROUP
    done_v = done.rearrange("(n p j i) c -> n p (j i c)", i=2, p=PP, j=PJ)

    ctx = ExitStack()
    with ctx:
        def sb(name, shape, dt=fp32):
            return ctx.enter_context(nc.sbuf_tensor(name, shape, dt))

        def sem(name):
            return ctx.enter_context(nc.semaphore(name))

        taken = {}

        def part_of(t, p, *shape):
            n = 1
            for d in shape:
                n *= d
            at = taken.get(t.name, 0)
            taken[t.name] = at + n
            names = "abc"[:len(shape)]
            dims = {k: d for k, d in zip(names, shape)}
            return t[0:p, at:at + n].rearrange(f"p ({' '.join(names)}) -> p {' '.join(names)}", **dims)
        X = sb("X", [P, XBUF * HW])
        Z = sb("Z", [P, ZBUF * HW])
        S1 = sb("S1", [P, 2, HP, WP], bf16)
        X2 = sb("X2", [P, TILES * P])
        ROWS = sb("ROWS", [P, 2, SLOTS, ROW])
        SQ = sb("SQ", [P, 2, CW])
        N1 = sb("N1", [P, 2, CW])
        N2 = sb("N2", [P, 2, CW])
        S2 = sb("S2", [P, 2, CW], bf16)
        VAR1 = sb("VAR1", [2 * NCH, CW])
        RA1 = sb("RA1", [2 * NCH, CW])
        RB1 = sb("RB1", [2 * NCH, CW])
        RSTD1 = sb("RSTD1", [2 * NCH, CW])
        SSQ = sb("SSQ", [P, SLOTS])
        SQR = sb("SQR", [P, 2 * RGROUP, C])
        LOGS = sb("LOGS", [P, TILES, GW - P])
        var2, r0, ra, rb = (sb(n, [P, SLOTS]) for n in ("var2", "r0", "ra", "rb"))
        mx, imin, ssum, prob, rowid, posn = (
            sb(n, [P, SLOTS]) for n in ("mx", "imin", "ssum", "prob", "rowid", "posn"))
        logit = sb("logit", [P, SLOTS, E])
        shifted = sb("shifted", [P, SLOTS, E])
        expo = sb("expo", [P, SLOTS, E])
        cand = sb("cand", [P, SLOTS, E])
        rowsel = sb("rowsel", [P, SLOTS, E])
        onehot = sb("onehot", [P, SLOTS, E], bf16)
        tile_tot = sb("tile_tot", [SLOTS, E], bf16)
        tile_off = sb("tile_off", [SLOTS, SLOTS, E], bf16)
        idx = sb("idx", [P, 2, SLOTS], u32)
        base = sb("base", [P, E])
        tokf = sb("tokf", [P, SLOTS])

        ident = sb("ident", [P, P])
        rowsel_w = sb("row_weights", [P, GW])
        center, gate = rowsel_w[:, 0:P], rowsel_w[:, P:GW]
        pick_var = sb("pick_var", [P, NCH, 2 * NCH])
        pick_bc = sb("pick_bc", [2 * NCH, NCH, P])
        upper = sb("upper", [P, P], bf16)
        ones = sb("ones", [P, P], bf16)
        earlier = sb("earlier", [SLOTS, SLOTS], bf16)
        iota8 = sb("iota8", [P, E])
        region0 = sb("region0", [P, E])
        gw2 = sb("gw2", [P, E])
        gb = sb("gb", [P, E])
        WB = sb("WB", [P, TAPS + 1, P], bf16)
        W3 = part_of(X2, P, C * TAPS)
        ABSW = part_of(X2, P, C * TAPS)
        SW = part_of(X2, P, TAPS + 1, P)
        WPW = sb("WPW", [P, C])
        ABSP = sb("ABSP", [P, C])
        PARAMS = ("va1", "va2", "g1", "g2", "be1", "be2", "mu1", "mu2",
                  "pm1", "pm2", "pb1", "pb2", "ps1", "ps2", "move1", "move2")
        NPAR = len(PARAMS)
        PROWS = NPAR + E * HC + E
        prow = sb("prow", [PROWS, P])
        par = sb("par", [P, PROWS])
        cst = sb("cst", [P, 32])

        RT = part_of(X, P, RING, SUB, ROW)
        XN = sb("XN", [P, 2, SUB, C])
        XT = sb("XT", [P, 2, DUO])
        HB = part_of(X, P, 2, HC, DUO)
        WALL = part_of(Z, P, E, WCOLS)
        WR = part_of(X, P, WRING, WCOLS)
        YS = sb("YS", [P, 2, DUO])
        Y2 = sb("Y2", [P, SUB, C])
        SGN = sb("SGN", [P, SUB, C])
        Y3 = sb("Y3", [P, SUB, C])
        TOKS = sb("TOKS", [P, SUB, C])
        FINITE = sb("FINITE", [P, SUB, C], i32)
        RES = part_of(X, P, RING, SUB, C)
        PAD = sb("PAD", [P, SUB, ROW])
        kio = sb("kio", [1, NSUP])
        tb = sb("tb", [1, 2, NSUP])
        tbe = sb("tbe", [1, 2, NSUP])
        tbi = sb("tbi", [1, 2, NSUP], i32)
        ind = sb("ind", [1, NSUP])
        ends = sb("ends", [1, E])
        endi = sb("endi", [1, E], i32)
        ntf = sb("ntf", [1, E])
        nti = sb("nti", [1, E], i32)
        ntp = sb("ntp", [1, E])
        ntd = sb("ntd", [1, E])

        bank = [ctx.enter_context(nc.psum_tensor(f"bank{n}", [P, 512], fp32)) for n in range(8)]
        MIX, VARP, CONV, PW, TRP, PRE = bank[0], bank[1], bank[2:4], bank[4], bank[5:7], bank[7]
        TOT0, SUM0 = SLOTS * E, SLOTS * E + E

        s_param = sem("param_loaded")
        s_gate = sem("gate_loaded")
        s_w = sem("conv_weights_loaded")
        s_fill = sem("constants_filled")
        s_zero = sem("zeroed")
        s_absw = sem("abs_weights")
        s_sgn = sem("sign_weights")
        s_setp = sem("setup_products")
        s_setr = sem("setup_read")
        s_setstep = sem("setup_step")
        s_setsd = sem("setup_sqrt")
        s_const = sem("channel_constants")
        s_x = [sem("x_even_loaded"), sem("x_odd_loaded")]
        s_cen = sem("centered")
        s_xc = sem("centered_copied")
        s_sq = sem("squared")
        s_vp = sem("variance_partial")
        s_v1 = sem("variance_read")
        s_sd1 = sem("rstd_guess_ready")
        s_nw = sem("newton_step")
        s_r1 = sem("rstd_ready")
        s_bc = sem("rstd_spread")
        s_xn = sem("normalized")
        s_s1 = sem("sign1_ready")
        s_cv = sem("conv_done")
        s_z1 = sem("sum1_ready")
        s_n1 = sem("negative1_ready")
        s_q1 = sem("prelu1_ready")
        s_s2 = sem("sign2_ready")
        s_pw = sem("pointwise_done")
        s_z2 = sem("sum2_ready")
        s_n2 = sem("negative2_ready")
        s_q2 = sem("prelu2_ready")
        s_x2 = sem("block_ready")
        s_tr = sem("rows_transposed")
        s_st = sem("row_stats_ready")
        s_lg = sem("logits_copied")
        s_lr = sem("logits_read")
        s_route = sem("route_step")
        s_rv = sem("row_variance")
        s_rs = sem("row_std")
        s_sh = sem("logits_shifted")
        s_ex = sem("exponentials")
        s_oh = sem("onehot_ready")
        s_tt = sem("tile_totals")
        s_of = sem("tile_offsets")
        s_pf = sem("prefix_ready")
        s_rr = sem("rows_routed")
        s_sc = [[sem(f"scattered_{'even' if k == 0 else 'odd'}_{g}") for g in range(NG)] for k in range(2)]
        s_pad = sem("padding_written")
        s_tab = sem("table_step")
        s_table = sem("table_ready")
        s_rt = [sem(f"super_rows_loaded_{k}") for k in range(RING)]
        s_wz = sem("expert_weights_zeroed")
        s_wall = sem("all_expert_weights_loaded")
        s_wr = sem("expert_weights_ready")
        s_ln = sem("rows_normalized")
        s_pt = sem("super_transposed")
        s_xt = sem("super_columns_copied")
        s_h = sem("hidden_done")
        s_ha = sem("hidden_relu_scalar")
        s_hb = sem("hidden_relu_vector")
        s_y = sem("expert_output")
        s_ys = sem("output_columns_copied")
        s_yb = sem("output_rows_transposed")
        s_g = sem("gating_step")
        s_res = sem("result_ready")
        s_back = [sem(f"results_scattered_{k}") for k in range(RING)]
        s_in3 = [sem("tokens_even_loaded"), sem("tokens_odd_loaded")]
        s_t3 = sem("images_transposed")
        s_c3 = sem("images_copied")
        s_past = sem("waits_passed")
        s_out = [sem("out_even_stored"), sem("out_odd_stored")]

        block = ctx.enter_context(nc.Block())

        FILLS = 21
        VAR_STEP = 3
        ROUTE_AT = (0, 0, 5, 10, 11, 17)
        NROUTE = ROUTE_AT[-1]
        GSTEPS = 5

        def wait(eng, s, count):
            if isinstance(count, int) and count <= 0:
                return
            eng.wait_ge(s, count)

        def wait_apart(eng, s, count):
            wait(eng, s, count)
            if not isinstance(count, int):
                eng.sem_inc(s_past, 1)

        def super_tiles(eng, first, end, one):
            passes = (end - first) // RING
            with eng.Fori(0, passes) as n:
                for u in range(RING):
                    one(n * RING + (first + u), (first + u) % RING)
            for k in range(first + passes * RING, end):
                one(k, k % RING)

        class Pair:
            def __init__(self, n, odd):
                self.n, self.odd = n, odd

            def x(self, c=0, width=HW):
                return ds((self.n % XBUF) * HW + c, width)

            def z(self, c=0, width=CW):
                return ds((self.n % ZBUF) * HW + c, width)

        def software_pipeline(eng, stage):
            def run(i, odd):
                pick = lambda k: Pair(i + k, (odd + k) % 2)
                static = isinstance(i, int)
                ok = lambda k: not static or 0 <= i + k < PAIRS
                stage(*(pick(k) if ok(k) else None for k in (2, 1, 0, -1)))
            for i in (-2, -1, 0, 1):
                run(i, i % 2)
            with eng.Fori(0, PAIRS // 2 - 2) as n:
                run(n * 2 + 2, 0)
                run(n * 2 + 3, 1)
            for i in range(PAIRS - 2, PAIRS + 1):
                run(i, i % 2)

        def T3(odd):
            w = 2 * PJ * C
            return Z[0:PP, odd * w:odd * w + w]

        INV, BIAS, ABSM, S_, OMS = 0, 2, 4, 6, 8
        B1P, NB1P, CA, SG2, B2P, NB2P, CB, TS, TA, TBB = 10, 11, 12, 13, 14, 15, 16, 18, 20, 22
        col = lambda k, n=1: cst[:, k:k + n]
        prm = lambda name, n=1: par[:, PARAMS.index(name):PARAMS.index(name) + n]

        @block.gpsimd
        def _(pool):
            n = [0]

            def step(ins):
                n[0] += 1
                ins.then_inc(s_fill, 1)

            def fence():
                pool.wait_ge(s_fill, n[0])
            for t, v in ((ident, 0.0), (pick_var, 0.0), (pick_bc, 0.0), (upper, 1.0), (ones, 1.0),
                         (earlier, 1.0), (PAD, 0.0), (rowsel_w, 0.0)):
                step(pool.memset(t[:], v))
            fence()
            for h in range(2):
                step(pool.memset(center[h * C:h * C + C, h * C:h * C + C], -1.0 / C))
            fence()
            step(pool.affine_select(out=ident[:], in_=ident[:], compare_op=ALU.not_equal, fill=1.0,
                                    base=0, pattern=[[-1, P]], channel_multiplier=1))
            step(pool.affine_select(out=center[:], in_=center[:], compare_op=ALU.not_equal, fill=1.0 - 1.0 / C,
                                    base=0, pattern=[[-1, P]], channel_multiplier=1))
            step(pool.affine_select(out=upper[:], in_=upper[:], compare_op=ALU.is_ge, fill=0.0,
                                    base=0, pattern=[[1, P]], channel_multiplier=-1))
            step(pool.affine_select(out=earlier[:], in_=earlier[:], compare_op=ALU.is_gt, fill=0.0,
                                    base=0, pattern=[[1, SLOTS]], channel_multiplier=-1))
            for h in range(2):
                part = pick_var[h * C:h * C + C]
                fence()
                step(pool.affine_select(out=part, in_=part, compare_op=ALU.not_equal, fill=1.0 / C, base=h,
                                        pattern=[[2, NCH], [-1, 2 * NCH]], channel_multiplier=0))
            fence()
            v = pick_bc[:].rearrange("r c (h m) -> r c h m", h=2)
            step(pool.affine_select(out=v, in_=v, compare_op=ALU.not_equal, fill=1.0, base=0,
                                    pattern=[[-2, NCH], [-1, 2], [0, C]], channel_multiplier=1))
            step(pool.iota(iota8[:], pattern=[[1, E]], base=-E, channel_multiplier=0,
                           allow_small_or_imprecise_dtypes=True))
            step(pool.iota(tokf[:].rearrange("p (h k) -> p h k", h=2), pattern=[[1, 2], [2 * P, TILES]], base=0,
                           channel_multiplier=2, allow_small_or_imprecise_dtypes=True))
            step(pool.iota(kio[:], pattern=[[1, NSUP]], base=0, channel_multiplier=0,
                           allow_small_or_imprecise_dtypes=True))
            fence()
            step(pool.iota(PAD[:, :, TOKEN].bitcast(i32), pattern=[[0, SUB]], base=TOKENS, channel_multiplier=0))
            assert n[0] == FILLS

            def scatter_pair(p):
                wait_apart(pool, s_rr, p.n + 1)
                for g in range(NG):
                    for k in group_tiles[g]:
                        live = P if k < TILES - 1 else LAST
                        for h in range(2):
                            s = h * TILES + k
                            pool.indirect_dma_start(
                                rows, bass.IndirectOffsetOnAxis(ap=idx[0:live, p.odd, s:s + 1], axis=0),
                                ROWS[0:live, p.odd, s, :], None).then_inc(s_sc[p.odd][g], 16)
            with pool.Fori(0, PAIRS // 2) as n_i:
                i = n_i * 2
                scatter_pair(Pair(i, 0))
                scatter_pair(Pair(i + 1, 1))

            def scatter_super(k, u):
                wait_apart(pool, s_res, k + 1)
                for j in range(SUB):
                    pool.indirect_dma_start(
                        done, bass.IndirectOffsetOnAxis(ap=RT[:, u, j, TOKEN:TOKEN + 1].bitcast(u32), axis=0),
                        RES[:, u, j, :], None, bounds_check=TOKENS - 1, oob_is_err=False,
                    ).then_inc(s_back[u], 16)
            super_tiles(pool, 0, NSUP, scatter_super)

        @block.sync
        def _(sp):
            for k, ap in enumerate((va1, va2, g1, g2, be1, be2, mu1, mu2)):
                sp.dma_start(prow[k:k + 1, 0:C], ap.rearrange("(a c) -> a c", a=1)).then_inc(s_param, 16)
            sp.dma_start(prow[NPAR:NPAR + E * HC, 0:C], b1.rearrange("e (q m) -> (e q) m", m=C)).then_inc(s_param, 16)
            sp.dma_start(prow[NPAR + E * HC:PROWS, 0:C], b2).then_inc(s_param, 16)
            for h in range(2):
                sp.dma_start(W3[h * C:h * C + C, :], w3.rearrange("o i a b -> o (i a b)")).then_inc(s_w, 16)
                sp.dma_start(WPW[h * C:h * C + C, :], w_pw.rearrange("o i a b -> o (i a b)")).then_inc(s_w, 16)

            def load(p):
                sp.dma_start(X[:, p.x()], x_v[ds(p.n, 1)].rearrange("a p m -> (a p) m")).then_inc(s_x[p.odd], 16)
            load(Pair(0, 0))
            load(Pair(1, 1))
            for k in (2, 3):
                sp.wait_ge(s_x[k % 2], 16)
                load(Pair(k, k % 2))
            with sp.Fori(0, (PAIRS - XBUF) // 2) as n_i:
                i = n_i * 2 + XBUF
                for k in range(2):
                    wait(sp, s_x2, (i + k - XBUF + 1) * NCH)
                    load(Pair(i + k, k))
            sp.wait_ge(s_wz, 1)
            for e in range(E):
                for h in range(2):
                    b = slice(h * C, h * C + C)
                    blocks = lambda at: WALL[b, e, at:at + HC * P].rearrange("p (q m) -> p q m", m=P)[:, :, b]
                    sp.dma_start(blocks(0), w1[e].rearrange("c (q m) -> c q m", m=C)).then_inc(s_wall, 16)
                    sp.dma_start(blocks(W2_AT), w2[e].rearrange("(q m) d -> m q d", m=C)).then_inc(s_wall, 16)
            sp.wait_ge(s_fill, FILLS)
            pad_rows = lambda at: rows[ds(at, SUPER), :].rearrange("(p j) c -> p j c", j=SUB)
            sp.dma_start(pad_rows(IDLE), PAD[:]).then_inc(s_pad, 16)
            sp.wait_ge(s_table, 1)
            for e in range(E):
                end = sp.value_load(endi[0:1, e:e + 1], min_val=e * REGION, max_val=e * REGION + TOKENS)
                sp.dma_start(pad_rows(end), PAD[:]).then_inc(s_pad, 16)
            sp.wait_ge(s_pad, 16 * (E + 1))
            for k in range(2):
                for g in range(NG):
                    sp.wait_ge(s_sc[k][g], 16 * 2 * len(group_tiles[g]) * (PAIRS // 2))

            def super_tile(k, u, first):
                at = sp.value_load(tbi[0:1, 0, ds(k, 1)], min_val=0, max_val=IDLE)
                if not first:
                    wait(sp, s_back[u], (k - u) * (16 * SUB // RING))
                sp.dma_start(RT[:, u], pad_rows(at)).then_inc(s_rt[u], 16)
            for u in range(RING):
                super_tile(u, u, True)
            super_tiles(sp, RING, NSUP, lambda k, u: super_tile(k, u, False))

            for u in range(RING):
                sp.wait_ge(s_back[u], 16 * SUB * len(range(u, NSUP, RING)))

            def load3(q, odd):
                sp.dma_start(T3(odd), done_v[ds(q, 1)].rearrange("a p m -> (a p) m")).then_inc(s_in3[odd], 16)

            def store3(q, odd):
                wait(sp, s_c3, NG3 * (q + 1))
                sp.dma_start(out_v[ds(q, 1)].rearrange("a p m -> (a p) m"),
                             X[:, odd * HW:odd * HW + HW]).then_inc(s_out[odd], 16)
            load3(0, 0)
            load3(1, 1)
            with sp.Fori(0, (PAIRS - 2) // 2) as n_q:
                q = n_q * 2
                for k in range(2):
                    store3(q + k, k)
                    load3(q + 2 + k, k)
            for k in range(2):
                store3(PAIRS - 2 + k, k)
            for k in range(2):
                sp.wait_ge(s_out[k], 16 * PAIRS // 2)

        @block.tensor
        def _(pe):
            mm = nc.tensor.matmul
            pe.wait_ge(s_fill, FILLS)
            pe.wait_ge(s_setstep, 1)
            nc.tensor.transpose(MIX[0:P, 0:PROWS], prow[:, :], ident[0:PROWS, 0:PROWS]).then_inc(s_setp, 1)
            pe.wait_ge(s_gate, 48)
            mm(VARP[:, 0:E], center[:, :], gw2[:, :], start=True, stop=True).then_inc(s_setp, 1)
            pe.wait_ge(s_sgn, 4)
            for t0 in range(0, TAPS + 1, GROUP):
                bk = (CONV[0], CONV[1], PW)[t0 // GROUP]
                for t in range(t0, min(t0 + GROUP, TAPS + 1)):
                    last = nc.tensor.transpose(bk[:, (t - t0) * P:(t - t0 + 1) * P], SW[:, t, :], ident[:, :])
                last.then_inc(s_setp, 1)
            pe.wait_ge(s_const, 1)

            def one_pass(cen, nor, con, rou):
                for c in range(NCH + 2):
                    if rou and c == 3:
                        wait(pe, s_oh, rou.n + 1)
                        for e in range(E):
                            last = mm(PRE[0:SLOTS, TOT0 + e:TOT0 + e + 1], onehot[:, :, e], ones[:, 0:1],
                                      start=True, stop=True)
                        last.then_inc(s_tt, 1)
                    if rou and c == 4:
                        wait(pe, s_of, rou.n + 1)
                        mm(PRE[:, SUM0:SUM0 + E], ones[0:SLOTS, :], tile_tot[:, :], start=True, stop=True)
                        mm(PRE[:, 0:SLOTS * E], upper[:, :], onehot[:].rearrange("p s e -> p (s e)"),
                           start=True, stop=False)
                        mm(PRE[:, 0:SLOTS * E], ones[0:SLOTS, :], tile_off[:].rearrange("p s e -> p (s e)"),
                           start=False, stop=True).then_inc(s_pf, 1)
                    if cen and c < NCH:
                        if c == 0:
                            wait(pe, s_x[cen.odd], (cen.n - cen.odd) * 8 + 16)
                        wait(pe, s_xn, (cen.n - 1) * NCH + c)
                        mm(MIX[:, 0:CW], center[:, :], X[:, cen.x(c * CW, CW)], start=True, stop=True).then_inc(s_cen, 1)
                    if con and c < NCH:
                        wait(pe, s_s1, con.n * NCH + min(c + 2, NCH))
                        wait(pe, s_z1, con.n * NCH + max(c - 1, 0))
                        for t in range(TAPS):
                            dy, dx = t // 3, t % 3
                            last = mm(CONV[c % 2][:, 0:CW], WB[:, t, :],
                                      S1[:, con.odd, c * CHUNK_ROWS + dy:(c + 1) * CHUNK_ROWS + dy, dx:dx + W],
                                      start=t == 0, stop=t == TAPS - 1)
                        last.then_inc(s_cv, 1)
                    if nor and c < NCH:
                        if c == 0:
                            wait(pe, s_r1, nor.n + 1)
                        wait(pe, s_sq, (nor.n + 1) * NCH + c + 1 if cen else PAIRS * NCH)
                        if not cen:
                            wait(pe, s_xn, nor.n * NCH + c)
                        mm(MIX[:, 0:CW], pick_bc[:, c, :], RSTD1[:, :], start=True, stop=True).then_inc(s_bc, 1)
                    if con and 1 <= c <= NCH:
                        wait(pe, s_s2, con.n * NCH + c)
                        wait(pe, s_z2, con.n * NCH + c - 1)
                        mm(PW[:, 0:CW], WB[:, TAPS, :], S2[:, (c - 1) % 2, :], start=True, stop=True).then_inc(s_pw, 1)
                    if cen and c < NCH:
                        wait(pe, s_sq, cen.n * NCH + c + 1)
                        if c == 0:
                            wait(pe, s_v1, cen.n)
                        mm(VARP[0:2 * NCH, 0:CW], pick_var[:, c, :], SQ[:, c % 2, :],
                           start=c == 0, stop=c == NCH - 1).then_inc(s_vp, 1)
                    if con:
                        for g in range(NG):
                            if min(last_chunk[g] + 2, NCH + 1) != c:
                                continue
                            wait(pe, s_x2, con.n * NCH + last_chunk[g] + 1)
                            wait(pe, s_st, con.n * NG + g - 1)
                            for k in group_tiles[g]:
                                at = k % RGROUP * GW
                                last = mm(TRP[(g + con.odd * NG) % 2][:, at:at + GW], X2[:, k * P:(k + 1) * P],
                                          rowsel_w[:, :], start=True, stop=True)
                            last.then_inc(s_tr, 1)
            software_pipeline(pe, one_pass)

            PT, HA, HV, YT, YB = bank[0:2], bank[2:4], bank[4], bank[5:7], bank[7]

            def super_pass(k, ring, t=True, l1=True, l2=True, back=True):
                if t:
                    b = (ring + 1) % 2
                    wait(pe, s_ln, k + 2)
                    wait_apart(pe, s_xt, k)
                    for d in range(DUO // P):
                        last = nc.tensor.transpose(PT[b][:, d * P:(d + 1) * P],
                                                   XN[:, b, 2 * d:2 * d + 2, :].rearrange("p i c -> p (i c)"), ident[:, :])
                    last.then_inc(s_pt, 1)
                if l1:
                    wait(pe, s_wr, k + 1)
                    wait(pe, s_xt, k + 1)
                    wait(pe, s_ha, k)
                    wait(pe, s_hb, k)
                    for q in range(HC):
                        to = HV[:, 0:DUO] if q == HC - 1 else HA[q // 2][:, (q % 2) * DUO:(q % 2 + 1) * DUO]
                        mm(to, WR[:, ring % WRING, q * P:(q + 1) * P], XT[:, ring % 2, :],
                           start=True, stop=True).then_inc(s_h, 1)
                if l2:
                    b = (ring - 1) % RING
                    wait(pe, s_ha, k)
                    wait(pe, s_hb, k)
                    wait(pe, s_ys, k - 2)
                    for q in range(HC):
                        at = W2_AT + q * P
                        last = mm(YT[b % 2][:, 0:DUO], WR[:, b % WRING, at:at + P], HB[:, b % 2, q, :],
                                  start=q == 0, stop=q == HC - 1)
                    last.then_inc(s_y, 1)
                if back:
                    b = ring % 2
                    wait(pe, s_ys, k - 1)
                    wait_apart(pe, s_g, (k - 3) * GSTEPS + 1)
                    for d in range(DUO // P):
                        last = nc.tensor.transpose(YB[:, d * P:(d + 1) * P], YS[:, b, d * P:(d + 1) * P], ident[:, :])
                    last.then_inc(s_yb, 1)
            super_pass(-1, -1 % RING, l1=False, l2=False, back=False)
            super_pass(0, 0, l2=False, back=False)
            super_pass(1, 1, back=False)
            super_pass(2, 2)
            super_tiles(pe, 3, NSUP - 1, super_pass)
            super_pass(NSUP - 1, (NSUP - 1) % RING, t=False)
            super_pass(NSUP, NSUP % RING, t=False, l1=False)
            super_pass(NSUP + 1, (NSUP + 1) % RING, t=False, l1=False, l2=False)

            def images(q, odd):
                wait(pe, s_in3[odd], (q - odd) * 8 + 16)
                for g in range(NG3):
                    wait(pe, s_c3, (q - 1) * NG3 + g + 1)
                    for j in range(GROUP):
                        t = (g * GROUP + j) * P
                        last = nc.tensor.transpose(bank[g][:, j * PP:(j + 1) * PP],
                                                   T3(odd)[:, t:t + P], ident[0:PP, 0:PP])
                    last.then_inc(s_t3, 1)
            images(0, 0)
            images(1, 1)
            with pe.Fori(0, (PAIRS - 2) // 2) as n_q:
                q = n_q * 2 + 2
                images(q, 0)
                images(q + 1, 1)

        @block.scalar
        def _(act):
            A = nc.scalar.activation
            for k, ap in enumerate((pm1, pm2, pb1, pb2, ps1, ps2, move1, move2)):
                act.dma_start(prow[8 + k:9 + k, 0:C], ap.rearrange("(a c) -> a c", a=1)).then_inc(s_param, 16)
            for h in range(2):
                act.dma_start(gw2[h * C:h * C + C, :], gate_w).then_inc(s_gate, 16)
            act.dma_start(gb[:, :], gate_b.rearrange("(a e) -> a e", a=1).to_broadcast([P, E])).then_inc(s_gate, 16)
            act.wait_ge(s_w, 64)
            A(ABSW[:, :], W3[:, :], ACT.Abs).then_inc(s_absw, 1)
            A(ABSP[:, :], WPW[:, :], ACT.Abs).then_inc(s_absw, 1)
            act.wait_ge(s_zero, 1)
            for h in range(2):
                b = slice(h * C, h * C + C)
                A(SW[b, 0:TAPS, b], W3[b, :].rearrange("o (i t) -> o t i", t=TAPS), ACT.Sign).then_inc(s_sgn, 1)
                A(SW[b, TAPS, b], WPW[b, :], ACT.Sign).then_inc(s_sgn, 1)
            act.wait_ge(s_setstep, VAR_STEP)
            A(col(TS, 2), col(TA, 2), ACT.Abs_reciprocal_sqrt).then_inc(s_setsd, 1)
            act.wait_ge(s_const, 1)

            def one_pass(cen, nor, con, rou):
                for c in range(NCH + 2):
                    if cen and c < NCH:
                        wait(act, s_cen, cen.n * NCH + c + 1)
                        wait_apart(act, s_x2, (cen.n - ZBUF) * NCH + c + 1)
                        A(Z[:, cen.z(c * CW)], MIX[:, 0:CW], ACT.Copy).then_inc(s_xc, 1)
                        wait(act, s_vp, cen.n * NCH + c - 1)
                        A(SQ[:, c % 2, :], MIX[:, 0:CW], ACT.Square).then_inc(s_sq, 1)
                    if con and c < NCH:
                        wait_apart(act, s_z1, con.n * NCH + c + 1)
                        A(N1[:, c % 2, :], Z[:, con.z(c * CW)], ACT.Relu, bias=col(NB1P), scale=-1.0).then_inc(s_n1, 1)
                    if nor and c < NCH:
                        wait_apart(act, s_xn, nor.n * NCH + c + 1)
                        A(S1[:, nor.odd, 1 + c * CHUNK_ROWS:1 + (c + 1) * CHUNK_ROWS, 1:1 + W],
                          Z[:, nor.z(c * CW)].rearrange("p (r w) -> p r w", w=W), ACT.Sign,
                          bias=prm("move1")).then_inc(s_s1, 1)
                    if con and c < NCH:
                        wait_apart(act, s_q1, con.n * NCH + c + 1)
                        A(S2[:, c % 2, :], Z[:, con.z(c * CW)], ACT.Sign, bias=col(SG2)).then_inc(s_s2, 1)
                    if con and 1 <= c <= NCH:
                        wait_apart(act, s_z2, con.n * NCH + c)
                        A(N2[:, (c - 1) % 2, :], Z[:, con.z((c - 1) * CW)], ACT.Relu, bias=col(NB2P),
                          scale=-1.0).then_inc(s_n2, 1)
                    if con:
                        for g in range(NG):
                            if min(last_chunk[g] + 2, NCH + 1) != c:
                                continue
                            wait(act, s_tr, con.n * NG + g + 1)
                            n = len(group_tiles[g])
                            src = TRP[(g + con.odd * NG) % 2][:, 0:n * GW].rearrange("p (k w) -> p k w", w=GW)
                            if g == 0:
                                wait_apart(act, s_rv, con.n)
                                wait_apart(act, s_lr, con.n)
                            A(LOGS[:, g * RGROUP:g * RGROUP + n, :], src[:, :, P:GW], ACT.Copy).then_inc(s_lg, 1)
                            wait(act, s_sc[con.odd][g], (con.n - con.odd) * 16 * n)
                            dst = ROWS[:, con.odd].rearrange("p (h k) r -> p h k r", h=2)
                            for h in range(2):
                                A(dst[:, h, g * RGROUP:g * RGROUP + n, 0:C], src[:, :, h * C:h * C + C], ACT.Copy)
                            wait(act, s_st, con.n * NG + g)
                            for k in range(n):
                                for h in range(2):
                                    slot = h * TILES + g * RGROUP + k
                                    last = A(SQR[:, 2 * k + h, :], src[:, k, h * C:h * C + C], ACT.Square,
                                             accum_out=SSQ[:, slot:slot + 1])
                            last.then_inc(s_st, 1)
                    if rou and c == 0:
                        wait(act, s_rv, rou.n + 1)
                        A(r0[:, :], var2[:, :], ACT.Abs_reciprocal_sqrt).then_inc(s_rs, 1)
                    if rou and c == 1:
                        wait(act, s_sh, rou.n + 1)
                        A(expo[:], shifted[:], ACT.Exp).then_inc(s_ex, 1)
                    if cen and c == NCH - 1:
                        wait(act, s_v1, cen.n + 1)
                        A(RA1[:, :], VAR1[:, :], ACT.Abs_reciprocal_sqrt).then_inc(s_sd1, 1)
            software_pipeline(act, one_pass)

            PT, HA, YT = bank[0:2], bank[2:4], bank[5:7]

            def take_weights(k, slot):
                e = act.value_load(tbi[0:1, 1, ds(k, 1)], min_val=0, max_val=E - 1)
                wait_apart(act, s_ys, k - WRING + 1)
                A(WR[:, slot, :], WALL[:, ds(e, 1), :].rearrange("p a w -> p (a w)"), ACT.Copy).then_inc(s_wr, 1)

            def super_pass(k, ring, t=True, h=True, w=True, y=True):
                if t:
                    b = (ring + 1) % 2
                    wait(act, s_pt, k + 2)
                    wait(act, s_h, HC * k)
                    A(XT[:, b, :], PT[b][:, 0:DUO], ACT.Copy).then_inc(s_xt, 1)
                if h:
                    wait(act, s_y, k - 1)
                    for q in range(HC - 1):
                        wait(act, s_h, HC * k + min(q // 2 * 2 + 2, HC - 1))
                        last = A(HB[:, ring % 2, q, :], HA[q // 2][:, (q % 2) * DUO:(q % 2 + 1) * DUO], ACT.Relu,
                                 bias=WR[:, ring % WRING, B1_AT + q:B1_AT + q + 1])
                    last.then_inc(s_ha, 1)
                if w:
                    take_weights(k + 2, (ring + 2) % WRING)
                if y:
                    b = (ring - 1) % RING
                    wait(act, s_y, k)
                    wait_apart(act, s_yb, k - 2)
                    A(YS[:, b % 2, :], YT[b % 2][:, 0:DUO], ACT.Identity,
                      bias=WR[:, b % WRING, B2_AT:B2_AT + 1]).then_inc(s_ys, 1)
            act.wait_ge(s_wall, 16 * 4 * E)
            act.wait_ge(s_table, 1)
            take_weights(0, 0)
            super_pass(-1, -1 % RING, h=False, y=False)
            super_pass(0, 0, y=False)
            super_pass(1, 1)
            super_pass(2, 2)
            super_tiles(act, 3, NSUP - 2, super_pass)
            super_pass(NSUP - 2, (NSUP - 2) % RING, w=False)
            super_pass(NSUP - 1, (NSUP - 1) % RING, t=False, w=False)
            super_pass(NSUP, NSUP % RING, t=False, h=False, w=False)

            def copy_images(q, odd):
                wait(act, s_out[odd], (q - odd) * 8)
                for g in range(NG3):
                    wait(act, s_t3, q * NG3 + g + 1)
                    dst = X[:, odd * HW:odd * HW + HW].rearrange("p (t j) -> p j t", j=PJ)
                    A(dst[:, g * GROUP:(g + 1) * GROUP, :],
                      bank[g][:, 0:GROUP * PP].rearrange("p (j t) -> p j t", t=PP), ACT.Copy).then_inc(s_c3, 1)
            copy_images(0, 0)
            copy_images(1, 1)
            with act.Fori(0, PAIRS // 2 - 1) as n:
                copy_images(n * 2 + 2, 0)
                copy_images(n * 2 + 3, 1)

        @block.vector
        def _(dve):
            V = nc.vector
            n = [0]

            def step(ins):
                n[0] += 1
                ins.then_inc(s_setstep, 1)
                dve.wait_ge(s_setstep, n[0])
            V.memset(SW[:], 0.0).then_inc(s_zero, 1)
            V.memset(S1[:].bitcast(u32), 0)
            V.memset(X2[:, HW:], 0.0)
            V.memset(ROWS[:], 0.0)
            for e in range(E):
                V.memset(region0[:, e:e + 1], float(e * REGION - 1))
            dve.wait_ge(s_param, 16 * (NPAR + 2))
            step(V.tensor_copy(prow[:, C:P], prow[:, 0:C]))
            dve.wait_ge(s_setp, 1)
            step(V.tensor_copy(par[:, :], MIX[:, 0:PROWS]))
            step(V.tensor_scalar(col(TA, 2), prm("va1", 2), EPS_BN, None, ALU.add))
            assert n[0] == VAR_STEP
            step(V.tensor_copy(base[:, :], region0[:, :]))
            dve.wait_ge(s_absw, 2)
            step(V.tensor_reduce(col(ABSM), ABSW[:, :], AX.X, ALU.add))
            step(V.tensor_reduce(col(ABSM + 1), ABSP[:, :], AX.X, ALU.add))
            step(V.tensor_scalar(col(ABSM), col(ABSM), 1.0 / (C * TAPS), None, ALU.mult))
            step(V.tensor_scalar(col(ABSM + 1), col(ABSM + 1), 1.0 / C, None, ALU.mult))
            dve.wait_ge(s_setsd, 1)
            step(V.tensor_tensor(col(TBB, 2), col(TS, 2), col(TS, 2), ALU.mult))
            step(V.scalar_tensor_tensor(out=col(TBB, 2), in0=col(TBB, 2), scalar=-0.5, in1=col(TA, 2), op0=ALU.mult, op1=ALU.mult))
            step(V.scalar_tensor_tensor(out=col(TS, 2), in0=col(TBB, 2), scalar=1.5, in1=col(TS, 2), op0=ALU.add, op1=ALU.mult))
            step(V.tensor_tensor(col(INV, 2), col(TS, 2), prm("g1", 2), ALU.mult))
            step(V.tensor_tensor(col(S_, 2), col(INV, 2), col(ABSM, 2), ALU.mult))
            step(V.tensor_tensor(col(BIAS, 2), prm("mu1", 2), col(INV, 2), ALU.mult))
            step(V.tensor_tensor(col(BIAS, 2), prm("be1", 2), col(BIAS, 2), ALU.subtract))
            step(V.tensor_scalar(col(OMS, 2), prm("ps1", 2), -1.0, 1.0, ALU.mult, ALU.add))
            step(V.tensor_tensor(col(B1P), col(BIAS), prm("pm1"), ALU.add))
            step(V.tensor_scalar(col(NB1P), col(B1P), -1.0, None, ALU.mult))
            step(V.tensor_tensor(col(CA), col(B1P), prm("pb1"), ALU.add))
            step(V.tensor_tensor(col(SG2), col(CA), prm("move2"), ALU.add))
            step(V.tensor_tensor(col(B2P), col(BIAS + 1), col(CA), ALU.add))
            step(V.tensor_tensor(col(B2P), col(B2P), prm("pm2"), ALU.add))
            step(V.tensor_scalar(col(NB2P), col(B2P), -1.0, None, ALU.mult))
            step(V.tensor_tensor(col(CB), col(B2P), prm("pb2"), ALU.add))
            dve.wait_ge(s_setp, 5)
            dve.wait_ge(s_fill, FILLS)
            for h in range(2):
                step(V.tensor_copy(gate[h * C:h * C + C, h * E:h * E + E], VARP[h * C:h * C + C, 0:E]))
                step(V.memset(gate[h * C:h * C + C, ME + h:ME + h + 1], 1.0 / C))
            for t0 in range(0, TAPS + 1, GROUP):
                t1 = min(t0 + GROUP, TAPS + 1)
                bk = (CONV[0], CONV[1], PW)[t0 // GROUP]
                step(V.tensor_copy(WB[:, t0:t1, :], bk[:, 0:(t1 - t0) * P].rearrange("p (t m) -> p t m", m=P)))
            V.memset(cst[:, 30:31], 0.0).then_inc(s_const, 1)

            over = lambda ap, m: ap.unsqueeze(1).to_broadcast([P, SLOTS, m])
            spread = lambda ap: ap.unsqueeze(2).to_broadcast([P, SLOTS, E])
            flat = lambda t: t[:].rearrange("p s e -> p (s e)")
            def route(p, c):
                r = [ROUTE_AT[c]]

                def op(ins, s=None):
                    if s is not None:
                        ins.then_inc(s, 1)
                        return
                    r[0] += 1
                    ins.then_inc(s_route, 1)
                    wait(dve, s_route, p.n * NROUTE + r[0])
                if c == 0:
                    wait(dve, s_st, (p.n + 1) * NG)
                    V.tensor_copy(ROWS[:, p.odd, :, MEAN].rearrange("p (h k) -> p h k", h=2),
                                  LOGS[:, :, ME:ME + 2].rearrange("p k h -> p h k"))
                    op(V.tensor_scalar(var2[:], SSQ[:], 1.0 / C, EPS_T, ALU.mult, ALU.add), s_rv)
                if c == 1:
                    wait(dve, s_rs, p.n + 1)
                    op(V.tensor_tensor(ra[:], r0[:], r0[:], ALU.mult))
                    op(V.scalar_tensor_tensor(out=rb[:], in0=ra[:], scalar=-0.5, in1=var2[:], op0=ALU.mult, op1=ALU.mult))
                    rstd = ROWS[:, p.odd, :, RSTD]
                    op(V.scalar_tensor_tensor(out=rstd, in0=rb[:], scalar=1.5, in1=r0[:], op0=ALU.add, op1=ALU.mult))
                    for h in range(2):
                        sl = slice(h * TILES, (h + 1) * TILES)
                        ins = V.tensor_tensor(
                            logit[:, sl, :], LOGS[:, :, h * E:h * E + E],
                            ROWS[:, p.odd, sl, RSTD:RSTD + 1].to_broadcast([P, TILES, E]), ALU.mult)
                    ins.then_inc(s_lr, 1)
                    wait(dve, s_lr, p.n + 1)
                    op(V.tensor_tensor(logit[:], logit[:], over(gb[:, :], E), ALU.add))
                    op(V.tensor_reduce(mx[:], logit[:], AX.X, ALU.max))
                    op(V.tensor_tensor(shifted[:], logit[:], spread(mx[:]), ALU.subtract), s_sh)
                if c == 2:
                    wait(dve, s_sh, p.n + 1)
                    op(V.scalar_tensor_tensor(out=cand[:], in0=shifted[:], scalar=0.0, in1=over(iota8[:, :], E),
                                              op0=ALU.is_ge, op1=ALU.mult))
                    op(V.tensor_reduce(imin[:], cand[:], AX.X, ALU.min))
                    op(V.tensor_tensor(onehot[:], over(iota8[:, :], E), spread(imin[:]), ALU.is_equal))
                    op(V.memset(onehot[LAST:P].rearrange("p (h k) e -> p h k e", h=2)[:, :, TILES - 1, :], 0.0), s_oh)
                    wait(dve, s_ex, p.n + 1)
                    op(V.tensor_reduce(ssum[:], expo[:], AX.X, ALU.add))
                    op(V.reciprocal(prob[:], ssum[:]))
                if c == 3:
                    wait(dve, s_tt, p.n + 1)
                    op(V.tensor_copy(tile_tot[:, :], PRE[0:SLOTS, TOT0:TOT0 + E]))
                    op(V.tensor_tensor(tile_off[:], earlier[:, :].unsqueeze(2).to_broadcast([SLOTS, SLOTS, E]),
                                       tile_tot[:, :].unsqueeze(1).to_broadcast([SLOTS, SLOTS, E]), ALU.mult), s_of)
                if c == 4:
                    wait(dve, s_pf, p.n + 1)
                    op(V.tensor_tensor(rowsel[:], PRE[:, 0:SLOTS * E].rearrange("p (s e) -> p s e", e=E),
                                       over(base[:, :], E), ALU.add))
                    op(V.tensor_tensor(base[:, :], base[:, :], PRE[:, SUM0:SUM0 + E], ALU.add))
                    op(V.tensor_tensor(rowsel[:], rowsel[:], onehot[:], ALU.mult))
                    op(V.tensor_reduce(rowid[:], rowsel[:], AX.X, ALU.add))
                    V.tensor_copy(idx[:, p.odd, :], rowid[:])
                    op(V.scalar_tensor_tensor(out=posn[:], in0=imin[:], scalar=-float(REGION), in1=rowid[:],
                                              op0=ALU.mult, op1=ALU.add))
                    V.tensor_copy(ROWS[:, p.odd, :, TOKEN].bitcast(u32), tokf[:])
                    op(V.scalar_tensor_tensor(out=ROWS[:, p.odd, :, GATE], in0=posn[:], scalar=float(E * REGION + CAPACITY),
                                              in1=prob[:], op0=ALU.is_lt, op1=ALU.mult))
                    V.tensor_scalar(tokf[:], tokf[:], float(2 * HW), None, ALU.add).then_inc(s_rr, 1)
                assert r[0] == ROUTE_AT[c + 1]

            def one_pass(cen, nor, con, rou):
                for c in range(NCH + 2):
                    if con and c < NCH:
                        wait(dve, s_cv, con.n * NCH + c + 1)
                        z = Z[:, con.z(c * CW)]
                        V.scalar_tensor_tensor(out=z, in0=CONV[c % 2][:, 0:CW], scalar=col(S_), in1=z,
                                               op0=ALU.mult, op1=ALU.add).then_inc(s_z1, 1)
                    if nor and c < NCH:
                        wait(dve, s_bc, nor.n * NCH + c + 1)
                        wait(dve, s_xc, nor.n * NCH + c + 1)
                        z = Z[:, nor.z(c * CW)]
                        V.tensor_tensor(z, z, MIX[:, 0:CW], ALU.mult).then_inc(s_xn, 1)
                    if con and c < NCH:
                        wait(dve, s_n1, con.n * NCH + c + 1)
                        z = Z[:, con.z(c * CW)]
                        V.scalar_tensor_tensor(out=z, in0=N1[:, c % 2, :], scalar=col(OMS), in1=z,
                                               op0=ALU.mult, op1=ALU.add).then_inc(s_q1, 1)
                    if con and 1 <= c <= NCH:
                        wait(dve, s_pw, con.n * NCH + c)
                        z = Z[:, con.z((c - 1) * CW)]
                        V.scalar_tensor_tensor(out=z, in0=PW[:, 0:CW], scalar=col(S_ + 1), in1=z,
                                               op0=ALU.mult, op1=ALU.add).then_inc(s_z2, 1)
                    if rou and c < 5:
                        route(rou, c)
                    if con and 1 <= c <= NCH:
                        wait(dve, s_n2, con.n * NCH + c)
                        z = Z[:, con.z((c - 1) * CW)]
                        V.scalar_tensor_tensor(out=z, in0=N2[:, (c - 1) % 2, :], scalar=col(OMS + 1), in1=z,
                                               op0=ALU.mult, op1=ALU.add).then_inc(s_q2, 1)
                    if con and 1 <= c <= NCH:
                        wait(dve, s_q2, con.n * NCH + c)
                        if c == 1:
                            wait(dve, s_tr, con.n * NG)
                        V.scalar_tensor_tensor(out=X2[:, (c - 1) * CW:c * CW], in0=Z[:, con.z((c - 1) * CW)],
                                               scalar=col(CB), in1=X[:, con.x((c - 1) * CW, CW)],
                                               op0=ALU.add, op1=ALU.add).then_inc(s_x2, 1)
                    if cen and c == NCH - 1:
                        wait(dve, s_vp, (cen.n + 1) * NCH)
                        V.tensor_scalar(VAR1[:, :], VARP[0:2 * NCH, 0:CW], EPS_C, None, ALU.add).then_inc(s_v1, 1)
                        wait(dve, s_sd1, cen.n + 1)
                        V.tensor_tensor(RB1[:, :], RA1[:, :], RA1[:, :], ALU.mult).then_inc(s_nw, 1)
                        wait(dve, s_nw, cen.n * 2 + 1)
                        V.scalar_tensor_tensor(out=RB1[:, :], in0=RB1[:, :], scalar=-0.5, in1=VAR1[:, :],
                                               op0=ALU.mult, op1=ALU.mult).then_inc(s_nw, 1)
                        wait(dve, s_nw, cen.n * 2 + 2)
                        wait(dve, s_bc, cen.n * NCH)
                        V.scalar_tensor_tensor(out=RSTD1[:, :], in0=RB1[:, :], scalar=1.5, in1=RA1[:, :],
                                               op0=ALU.add, op1=ALU.mult).then_inc(s_r1, 1)
            software_pipeline(dve, one_pass)

            m = [0]

            def tstep(ins):
                m[0] += 1
                ins.then_inc(s_tab, 1)
                dve.wait_ge(s_tab, m[0])
            dve.wait_ge(s_x2, PAIRS * NCH)
            tstep(V.memset(WALL[:], 0.0))
            tstep(V.tensor_copy(WALL[:, :, B1_AT:B1_AT + HC],
                                par[:, NPAR:NPAR + E * HC].rearrange("p (e q) -> p e q", q=HC)))
            V.tensor_copy(WALL[:, :, B2_AT], par[:, NPAR + E * HC:PROWS]).then_inc(s_wz, 1)
            dve.wait_ge(s_rr, PAIRS)
            tstep(V.tensor_scalar(ends[:, :], base[0:1, :], 1.0, None, ALU.add))
            tstep(V.tensor_copy(endi[:, :], ends[:, :]))
            tstep(V.tensor_tensor(ntf[:, :], base[0:1, :], region0[0:1, :], ALU.subtract))
            tstep(V.tensor_scalar(ntf[:, :], ntf[:, :], float(SUPER - 1), None, ALU.add))
            tstep(V.tensor_copy(nti[:, :], ntf[:, :]))
            tstep(V.tensor_scalar(nti[:, :], nti[:, :], SUPER.bit_length() - 1, None, ALU.arith_shift_right))
            tstep(V.tensor_copy(ntf[:, :], nti[:, :]))
            tstep(V.tensor_copy(ntp[:, :], ntf[:, :]))
            for e in range(1, E):
                tstep(V.tensor_tensor(ntp[:, e:e + 1], ntp[:, e:e + 1], ntp[:, e - 1:e], ALU.add))
            tstep(V.tensor_scalar(ntd[:, :], ntf[:, :], -float(SUPER), float(REGION), ALU.mult, ALU.add))
            tstep(V.tensor_scalar(tb[:, 0, :], kio[:, :], float(SUPER), None, ALU.mult))
            tstep(V.memset(tb[:, 1, :], 0.0))
            for e in range(E):
                tstep(V.tensor_scalar(ind[:, :], kio[:, :], ntp[:, e:e + 1], ntd[:, e:e + 1], ALU.is_ge, ALU.mult))
                tstep(V.tensor_tensor(tb[:, 0, :], tb[:, 0, :], ind[:, :], ALU.add))
                tstep(V.scalar_tensor_tensor(out=tb[:, 1, :], in0=kio[:, :], scalar=ntp[:, e:e + 1], in1=tb[:, 1, :],
                                             op0=ALU.is_ge, op1=ALU.add))
            tstep(V.tensor_scalar(tbe[:, 0, :], tb[:, 0, :], float(IDLE), None, ALU.min))
            tstep(V.tensor_scalar(tbe[:, 1, :], tb[:, 1, :], float(E - 1), None, ALU.min))
            V.tensor_copy(tbi[:], tbe[:]).then_inc(s_table, 1)

            HV, YB = bank[4], bank[7]

            def super_pass(k, ring, ln=True, h=True, fin=True):
                if ln:
                    u, b = (ring + 2) % RING, ring % 2
                    wait(dve, s_rt[u], (k + 2 - u) * (16 // RING) + 16)
                    wait(dve, s_pt, k + 1)
                    V.tensor_tensor(XN[:, b], RT[:, u, :, 0:C], RT[:, u, :, RSTD:RSTD + 1].to_broadcast([P, SUB, C]),
                                    ALU.mult).then_inc(s_ln, 1)
                if h:
                    wait(dve, s_h, HC * k + HC)
                    wait(dve, s_y, k - 1)
                    q = HC - 1
                    V.tensor_scalar(HB[:, ring % 2, q, :], HV[:, 0:DUO], WR[:, ring % WRING, B1_AT + q:B1_AT + q + 1],
                                    0.0, ALU.add, ALU.max).then_inc(s_hb, 1)
                if fin:
                    u = (ring - 2) % RING
                    g = [0]

                    def gstep(ins, wait=wait):
                        g[0] += 1
                        ins.then_inc(s_g, 1)
                        wait(dve, s_g, (k - 2) * GSTEPS + g[0])
                    wait(dve, s_yb, k - 1)
                    y = YB[:, 0:SUB * C].rearrange("p (j c) -> p j c", c=C)
                    gstep(V.tensor_tensor(Y2[:], y, RT[:, u, :, GATE:GATE + 1].to_broadcast([P, SUB, C]), ALU.mult))
                    V.tensor_tensor(TOKS[:], RT[:, u, :, 0:C], RT[:, u, :, MEAN:MEAN + 1].to_broadcast([P, SUB, C]), ALU.add)
                    V.tensor_scalar(FINITE[:], Y2[:], 0.0, 0.0, ALU.mult, ALU.is_equal)
                    gstep(V.tensor_scalar(SGN[:], Y2[:], 0.0, None, ALU.is_gt))
                    gstep(V.scalar_tensor_tensor(out=SGN[:], in0=Y2[:], scalar=0.0, in1=SGN[:], op0=ALU.is_lt, op1=ALU.subtract))
                    gstep(V.tensor_scalar(Y3[:], SGN[:], -LIMIT, None, ALU.mult), wait_apart)
                    gstep(V.copy_predicated(Y3[:], FINITE[:], Y2[:]))
                    assert g[0] == GSTEPS
                    V.tensor_tensor(RES[:, u], Y3[:], TOKS[:], ALU.add).then_inc(s_res, 1)
            super_pass(-2, -2 % RING, h=False, fin=False)
            super_pass(-1, -1 % RING, h=False, fin=False)
            super_pass(0, 0, fin=False)
            super_pass(1, 1, fin=False)
            super_pass(2, 2)
            super_tiles(dve, 3, NSUP - 2, super_pass)
            super_pass(NSUP - 2, (NSUP - 2) % RING, ln=False)
            super_pass(NSUP - 1, (NSUP - 1) % RING, ln=False)
            super_pass(NSUP, NSUP % RING, ln=False, h=False)
            super_pass(NSUP + 1, (NSUP + 1) % RING, ln=False, h=False)


_INS = ['x', 'L0_conv_move1_bias', 'L0_conv_w3', 'L0_conv_bn1_gamma', 'L0_conv_bn1_beta', 'L0_conv_bn1_mean',
        'L0_conv_bn1_var', 'L0_conv_prelu1_move', 'L0_conv_prelu1_slope', 'L0_conv_prelu1_bias', 'L0_conv_move2_bias',
        'L0_conv_w_pw', 'L0_conv_bn2_gamma', 'L0_conv_bn2_beta', 'L0_conv_bn2_mean', 'L0_conv_bn2_var',
        'L0_conv_prelu2_move', 'L0_conv_prelu2_slope', 'L0_conv_prelu2_bias', 'L0_ffn_gate_w', 'L0_ffn_gate_b',
        'L0_ffn_w1', 'L0_ffn_b1', 'L0_ffn_w2', 'L0_ffn_b2']


def kernel(**inputs):
    import numpy as _np
    import concourse.bacc as _bacc
    from concourse import mybir as _mybir
    from concourse.bass_utils import run_bass_kernel_spmd as _run

    nc = _bacc.Bacc("TRN2", target_bir_lowering=False, num_devices=1)
    arrays, args = {}, []
    for name in _INS:
        a = _np.ascontiguousarray(inputs[name])
        arrays[f"in_{name}_dram"] = a
        args.append(nc.dram_tensor(f"in_{name}_dram", a.shape, _mybir.dt.from_np(a.dtype), kind="ExternalInput").ap())
    shape = inputs['x'].shape
    args.append(nc.dram_tensor("out_0_dram", shape, _mybir.dt.float32, kind="ExternalOutput").ap())
    metaformer_kernel(nc, *args)
    r = _run(nc, [arrays], core_ids=[0])
    return r.results[0]["out_0_dram"]
```

```python
import concourse.bass as bass
from concourse import mybir
from contextlib import ExitStack


def metaformer_kernel(nc, x, move1, w3, g1, be1, mu1, va1, pm1, ps1, pb1, move2, w_pw,
                      g2, be2, mu2, va2, pm2, ps2, pb2, gate_w, gate_b, w1, b1, w2, b2, out):
    fp32, bf16 = mybir.dt.float32, mybir.dt.bfloat16
    i32, u32 = mybir.dt.int32, mybir.dt.uint32
    ALU, ACT, AX = mybir.AluOpType, mybir.ActivationFunctionType, mybir.AxisListType
    ds = bass.ds

    IMAGES, C, H, W = x.shape
    E, _, F = w1.shape
    HW = H * W
    PAIRS = IMAGES // 2
    P = 2 * C
    TOKENS = IMAGES * HW
    CAPACITY = -(-5 * TOKENS // (4 * E))
    CHUNK_ROWS = 8
    NCH = H // CHUNK_ROWS
    CW = CHUNK_ROWS * W
    TILES = -(-HW // P)
    LAST = HW - (TILES - 1) * P
    SLOTS = 2 * TILES
    assert 2 * LAST == P
    GROUP = 4
    RGROUP = 3
    NG = -(-TILES // RGROUP)
    ME = 2 * E
    GW = P + 2 * E + 2
    HP, WP = H + 2, W + 2
    TAPS = 9
    XBUF, ZBUF = 4, 3

    MEAN, RSTD, GATE, TOKEN = C, C + 1, C + 2, C + 3
    ROW = C + 4
    SUPER = 512
    SUB = SUPER // P
    REGION = TOKENS + SUPER
    IDLE = E * REGION
    NSUP = (TOKENS + E * (SUPER - 1)) // SUPER
    HC = F // C
    DUO = SUPER // 2
    WCOLS = 2 * HC * P + HC + 1
    W2_AT, B1_AT, B2_AT = HC * P, 2 * HC * P, 2 * HC * P + HC
    RING = 8
    WRING = 4
    EPS_C, EPS_T, EPS_BN = 1e-6, 1e-5, 1e-5
    LIMIT = 10000.0

    last_chunk = [min(((min((g + 1) * RGROUP * P, HW)) - 1) // CW, NCH - 1) for g in range(NG)]
    group_tiles = [list(range(g * RGROUP, min((g + 1) * RGROUP, TILES))) for g in range(NG)]
    assert group_tiles[-1] == [TILES - 1]
    scatters = [sum(1 if k == TILES - 1 else 2 for k in tiles) for tiles in group_tiles]
    group_slot = [min(c + 2, NCH + 1) for c in last_chunk]

    rows = nc.dram_tensor("rows_by_expert", (IDLE + SUPER, ROW), fp32).ap()
    done = nc.dram_tensor("rows_by_token", (TOKENS, C), fp32).ap()

    x_v = x.rearrange("(n i) c h w -> n (i c) (h w)", i=2)
    out_v = out.rearrange("(n i) c h w -> n (i c) (h w)", i=2)
    PJ = 28
    PP = HW // PJ
    NG3 = PJ // GROUP
    done_v = done.rearrange("(n p j i) c -> n p (j i c)", i=2, p=PP, j=PJ)

    ctx = ExitStack()
    with ctx:
        def sb(name, shape, dt=fp32):
            return ctx.enter_context(nc.sbuf_tensor(name, shape, dt))

        def sem(name):
            return ctx.enter_context(nc.semaphore(name))

        taken = {}

        def part_of(t, p, *shape):
            n = 1
            for d in shape:
                n *= d
            at = taken.get(t.name, 0)
            taken[t.name] = at + n
            names = "abc"[:len(shape)]
            dims = {k: d for k, d in zip(names, shape)}
            return t[0:p, at:at + n].rearrange(f"p ({' '.join(names)}) -> p {' '.join(names)}", **dims)
        X = sb("X", [P, XBUF * HW])
        Z = sb("Z", [P, ZBUF * HW])
        S1 = sb("S1", [P, 2, HP, WP], bf16)
        X2 = sb("X2", [P, TILES * P])
        ROWS = sb("ROWS", [P, 2, SLOTS, ROW])
        SQ = sb("SQ", [P, 2, CW])
        N1 = sb("N1", [P, 2, CW])
        N2 = sb("N2", [P, 2, CW])
        S2 = sb("S2", [P, 2, CW], bf16)
        VAR1 = sb("VAR1", [2 * NCH, CW])
        RA1 = sb("RA1", [2 * NCH, CW])
        RB1 = sb("RB1", [2 * NCH, CW])
        RSTD1 = sb("RSTD1", [2 * NCH, CW])
        SSQ = sb("SSQ", [P, 2, SLOTS])
        SQR = sb("SQR", [P, 2 * RGROUP, C])
        LOGS = sb("LOGS", [P, 2, TILES, GW - P])
        var2, r0, ra, rb = (sb(n, [P, SLOTS]) for n in ("var2", "r0", "ra", "rb"))
        mx, imin, ssum, prob, rowid, posn = (
            sb(n, [P, SLOTS]) for n in ("mx", "imin", "ssum", "prob", "rowid", "posn"))
        logit = sb("logit", [P, SLOTS, E])
        shifted = sb("shifted", [P, SLOTS, E])
        expo = sb("expo", [P, SLOTS, E])
        cand = sb("cand", [P, SLOTS, E])
        rowsel = sb("rowsel", [P, SLOTS, E])
        onehot = sb("onehot", [P, SLOTS, E], bf16)
        tile_tot = sb("tile_tot", [SLOTS, E], bf16)
        tile_off = sb("tile_off", [SLOTS, SLOTS, E], bf16)
        idx = sb("idx", [P, 2, SLOTS], u32)
        base = sb("base", [P, E])
        tokf = sb("tokf", [P, SLOTS])

        ident = sb("ident", [P, P])
        row_weights = sb("row_weights", [P, GW])
        center, gate = row_weights[:, 0:P], row_weights[:, P:GW]
        pick_var = sb("pick_var", [P, NCH, 2 * NCH])
        pick_bc = sb("pick_bc", [2 * NCH, NCH, P])
        upper = sb("upper", [P, P], bf16)
        ones = sb("ones", [P, P], bf16)
        earlier = sb("earlier", [SLOTS, SLOTS], bf16)
        iota8 = sb("iota8", [P, E])
        region0 = sb("region0", [P, E])
        gw2 = sb("gw2", [P, E])
        gb = sb("gb", [P, E])
        WB = sb("WB", [P, TAPS + 1, P], bf16)
        W3 = part_of(X2, P, C * TAPS)
        ABSW = part_of(X2, P, C * TAPS)
        SW = part_of(X2, P, TAPS + 1, P)
        WPW = sb("WPW", [P, C])
        ABSP = sb("ABSP", [P, C])
        PARAMS = ("va1", "va2", "g1", "g2", "be1", "be2", "mu1", "mu2",
                  "pm1", "pm2", "pb1", "pb2", "ps1", "ps2", "move1", "move2")
        NPAR = len(PARAMS)
        PROWS = NPAR + E * HC + E
        prow = sb("prow", [PROWS, P])
        par = sb("par", [P, PROWS])
        cst = sb("cst", [P, 32])

        RT = part_of(X, P, RING, SUB, ROW)
        XN = sb("XN", [P, 2, SUB, C])
        XT = sb("XT", [P, 2, DUO])
        HB = part_of(X, P, 2, HC, DUO)
        WALL = part_of(Z, P, E, WCOLS)
        WR = part_of(X, P, WRING, WCOLS)
        YS = sb("YS", [P, 2, DUO])
        Y2 = sb("Y2", [P, SUB, C])
        SGN = sb("SGN", [P, SUB, C])
        Y3 = sb("Y3", [P, SUB, C])
        TOKS = sb("TOKS", [P, SUB, C])
        FINITE = sb("FINITE", [P, SUB, C], i32)
        RES = part_of(X, P, RING, SUB, C)
        PAD = sb("PAD", [P, SUB, ROW])
        kio = sb("kio", [1, NSUP])
        tb = sb("tb", [1, 2, NSUP])
        tbe = sb("tbe", [1, 2, NSUP])
        tbi = sb("tbi", [1, 2, NSUP], i32)
        ind = sb("ind", [1, NSUP])
        ends = sb("ends", [1, E])
        endi = sb("endi", [1, E], i32)
        ntf = sb("ntf", [1, E])
        nti = sb("nti", [1, E], i32)
        ntp = sb("ntp", [1, E])
        ntd = sb("ntd", [1, E])

        bank = [ctx.enter_context(nc.psum_tensor(f"bank{n}", [P, 512], fp32)) for n in range(8)]
        CEN, VARP, CONV, PW, SPREAD, PRE = bank[0], bank[1], bank[2:4], bank[4], bank[5], bank[7]
        second = [g > 0 and group_slot[g] == group_slot[g - 1] for g in range(NG)]
        ROWP = [PRE if second[g] else bank[6] for g in range(NG)]
        TOT0, SUM0 = SLOTS * E, SLOTS * E + E

        s_param = sem("param_loaded")
        s_gate = sem("gate_loaded")
        s_w = sem("conv_weights_loaded")
        s_fill = sem("constants_filled")
        s_zero = sem("zeroed")
        s_absw = sem("abs_weights")
        s_sgn = sem("sign_weights")
        s_setp = sem("setup_products")
        s_setstep = sem("setup_step")
        s_setsd = sem("setup_sqrt")
        s_const = sem("channel_constants")
        s_x = [sem("x_even_loaded"), sem("x_odd_loaded")]
        s_cen = sem("centered")
        s_xc = sem("centered_copied")
        s_sq = sem("squared")
        s_vp = sem("variance_partial")
        s_v1 = sem("variance_read")
        s_sd1 = sem("rstd_guess_ready")
        s_nw = sem("newton_step")
        s_r1 = sem("rstd_ready")
        s_bc = sem("rstd_spread")
        s_xn = sem("normalized")
        s_s1 = sem("sign1_ready")
        s_cv = sem("conv_done")
        s_z1 = sem("sum1_ready")
        s_n1 = sem("negative1_ready")
        s_q1 = sem("prelu1_ready")
        s_s2 = sem("sign2_ready")
        s_pw = sem("pointwise_done")
        s_z2 = sem("sum2_ready")
        s_n2 = sem("negative2_ready")
        s_q2 = sem("prelu2_ready")
        s_x2 = sem("block_ready")
        s_tr = sem("rows_transposed")
        s_st = sem("row_stats_ready")
        s_lr = sem("logits_read")
        s_route = sem("route_step")
        s_rv = sem("row_variance")
        s_rs = sem("row_std")
        s_sh = sem("logits_shifted")
        s_ex = sem("exponentials")
        s_oh = sem("onehot_ready")
        s_tt = sem("tile_totals")
        s_of = sem("tile_offsets")
        s_pf = sem("prefix_ready")
        s_rr = sem("rows_routed")
        s_sc = [[sem(f"scattered_{'even' if k == 0 else 'odd'}_{g}") for g in range(NG)] for k in range(2)]
        s_pad = sem("padding_written")
        s_tab = sem("table_step")
        s_table = sem("table_ready")
        s_rt = [sem(f"super_rows_loaded_{k}") for k in range(RING)]
        s_wz = sem("expert_weights_zeroed")
        s_wall = sem("all_expert_weights_loaded")
        s_wr = sem("expert_weights_ready")
        s_ln = sem("rows_normalized")
        s_pt = sem("super_transposed")
        s_xt = sem("super_columns_copied")
        s_h = sem("hidden_done")
        s_ha = sem("hidden_relu_scalar")
        s_hb = sem("hidden_relu_vector")
        s_y = sem("expert_output")
        s_ys = sem("output_columns_copied")
        s_yb = sem("output_rows_transposed")
        s_g = sem("gating_step")
        s_res = sem("result_ready")
        s_back = [sem(f"results_scattered_{k}") for k in range(RING)]
        s_in3 = [sem("tokens_even_loaded"), sem("tokens_odd_loaded")]
        s_t3 = sem("images_transposed")
        s_c3 = sem("images_copied")
        s_past = sem("waits_passed")
        s_out = [sem("out_even_stored"), sem("out_odd_stored")]

        block = ctx.enter_context(nc.Block())

        FILLS = 22
        GATE_AT = 3 * P
        VAR_STEP = 3
        ROUTE_AT = (0, 0, 5, 10, 11, 17)
        NROUTE = ROUTE_AT[-1]
        GSTEPS = 5

        def wait(eng, s, count):
            if isinstance(count, int) and count <= 0:
                return
            eng.wait_ge(s, count)

        def wait_apart(eng, s, count):
            wait(eng, s, count)
            if not isinstance(count, int):
                eng.sem_inc(s_past, 1)

        def super_tiles(eng, first, end, one):
            passes = (end - first) // RING
            with eng.Fori(0, passes) as n:
                for u in range(RING):
                    one(n * RING + (first + u), (first + u) % RING)
            for k in range(first + passes * RING, end):
                one(k, k % RING)

        class Pair:
            def __init__(self, n, odd):
                self.n, self.odd = n, odd

            def x(self, c=0, width=HW):
                return ds((self.n % XBUF) * HW + c, width)

            def z(self, c=0, width=CW):
                return ds((self.n % ZBUF) * HW + c, width)

        def software_pipeline(eng, stage, constants=None):
            def run(i, odd):
                pick = lambda k: Pair(i + k, (odd + k) % 2)
                static = isinstance(i, int)
                ok = lambda k: not static or 0 <= i + k < PAIRS
                stage(*(pick(k) if ok(k) else None for k in (2, 1, 0, -1)))
            run(-2, 0)
            if constants:
                eng.wait_ge(constants, 1)
            for i in range(-1, 4):
                run(i, i % 2)
            with eng.Fori(0, PAIRS // 2 - 3) as n:
                run(n * 2 + 4, 0)
                run(n * 2 + 5, 1)
            for i in range(PAIRS - 2, PAIRS + 1):
                run(i, i % 2)

        def T3(odd):
            w = 2 * PJ * C
            return Z[0:PP, odd * w:odd * w + w]

        def centered(c, alone):
            return SPREAD if alone and c % 2 else CEN

        INV, BIAS, ABSM, S_, OMS, SM1 = 0, 2, 4, 6, 8, 9
        B1P, CA, SG2, B2P, NB2P, CB, TS, TA, TBB = 10, 12, 13, 14, 15, 16, 18, 20, 22
        col = lambda k, n=1: cst[:, k:k + n]
        prm = lambda name, n=1: par[:, PARAMS.index(name):PARAMS.index(name) + n]

        @block.gpsimd
        def _(pool):
            n = [0]

            def step(ins):
                n[0] += 1
                ins.then_inc(s_fill, 1)

            def fence():
                pool.wait_ge(s_fill, n[0])
            for t, v in ((ident, 0.0), (pick_var, 0.0), (pick_bc, 0.0), (upper, 1.0), (ones, 1.0),
                         (earlier, 1.0), (PAD, 0.0), (row_weights, 0.0)):
                step(pool.memset(t[:], v))
            fence()
            for h in range(2):
                step(pool.memset(center[h * C:h * C + C, h * C:h * C + C], -1.0 / C))
            fence()
            step(pool.affine_select(out=ident[:], in_=ident[:], compare_op=ALU.not_equal, fill=1.0,
                                    base=0, pattern=[[-1, P]], channel_multiplier=1))
            step(pool.affine_select(out=center[:], in_=center[:], compare_op=ALU.not_equal, fill=1.0 - 1.0 / C,
                                    base=0, pattern=[[-1, P]], channel_multiplier=1))
            step(pool.affine_select(out=upper[:], in_=upper[:], compare_op=ALU.is_ge, fill=0.0,
                                    base=0, pattern=[[1, P]], channel_multiplier=-1))
            step(pool.affine_select(out=earlier[:], in_=earlier[:], compare_op=ALU.is_gt, fill=0.0,
                                    base=0, pattern=[[1, SLOTS]], channel_multiplier=-1))
            for h in range(2):
                part = pick_var[h * C:h * C + C]
                fence()
                step(pool.affine_select(out=part, in_=part, compare_op=ALU.not_equal, fill=1.0 / C, base=h,
                                        pattern=[[2, NCH], [-1, 2 * NCH]], channel_multiplier=0))
            fence()
            v = pick_bc[:].rearrange("r c (h m) -> r c h m", h=2)
            step(pool.affine_select(out=v, in_=v, compare_op=ALU.not_equal, fill=1.0, base=0,
                                    pattern=[[-2, NCH], [-1, 2], [0, C]], channel_multiplier=1))
            step(pool.iota(iota8[:], pattern=[[1, E]], base=-E, channel_multiplier=0,
                           allow_small_or_imprecise_dtypes=True))
            step(pool.iota(tokf[:].rearrange("p (h k) -> p h k", h=2), pattern=[[1, 2], [2 * P, TILES]], base=0,
                           channel_multiplier=2, allow_small_or_imprecise_dtypes=True))
            step(pool.iota(kio[:], pattern=[[1, NSUP]], base=0, channel_multiplier=0,
                           allow_small_or_imprecise_dtypes=True))
            fence()
            step(pool.iota(tokf[:, SLOTS - 1:SLOTS], pattern=[[0, 1]], base=2 * (HW - P) + 1, channel_multiplier=2,
                           allow_small_or_imprecise_dtypes=True))
            step(pool.iota(PAD[:, :, TOKEN].bitcast(i32), pattern=[[0, SUB]], base=TOKENS, channel_multiplier=0))
            assert n[0] == FILLS

            def scatter_pair(p):
                wait_apart(pool, s_rr, p.n + 1)
                for g in range(NG):
                    for k in group_tiles[g]:
                        for h in range(1 if k == TILES - 1 else 2):
                            s = h * TILES + k
                            pool.indirect_dma_start(
                                rows, bass.IndirectOffsetOnAxis(ap=idx[:, p.odd, s:s + 1], axis=0),
                                ROWS[:, p.odd, s, :], None).then_inc(s_sc[p.odd][g], 16)
            with pool.Fori(0, PAIRS // 2) as n_i:
                i = n_i * 2
                scatter_pair(Pair(i, 0))
                scatter_pair(Pair(i + 1, 1))

            def scatter_super(k, u):
                wait_apart(pool, s_res, k + 1)
                for j in range(SUB):
                    pool.indirect_dma_start(
                        done, bass.IndirectOffsetOnAxis(ap=RT[:, u, j, TOKEN:TOKEN + 1].bitcast(u32), axis=0),
                        RES[:, u, j, :], None, bounds_check=TOKENS - 1, oob_is_err=False,
                    ).then_inc(s_back[u], 16)
            super_tiles(pool, 0, NSUP, scatter_super)

        @block.sync
        def _(sp):
            def load(p):
                sp.dma_start(X[:, p.x()], x_v[ds(p.n, 1)].rearrange("a p m -> (a p) m")).then_inc(s_x[p.odd], 16)
            load(Pair(0, 0))
            for k, ap in enumerate((va1, va2, g1, g2, be1, be2, mu1, mu2)):
                sp.dma_start(prow[k:k + 1, 0:C], ap.rearrange("(a c) -> a c", a=1)).then_inc(s_param, 16)
            sp.dma_start(prow[NPAR:NPAR + E * HC, 0:C], b1.rearrange("e (q m) -> (e q) m", m=C)).then_inc(s_param, 16)
            sp.dma_start(prow[NPAR + E * HC:PROWS, 0:C], b2).then_inc(s_param, 16)
            for k, ap in enumerate((pm1, pm2, pb1, pb2, ps1, ps2, move1, move2)):
                sp.dma_start(prow[8 + k:9 + k, 0:C], ap.rearrange("(a c) -> a c", a=1)).then_inc(s_param, 16)
            for h in range(2):
                sp.dma_start(gw2[h * C:h * C + C, :], gate_w).then_inc(s_gate, 16)
            sp.dma_start(gb[:, :], gate_b.rearrange("(a e) -> a e", a=1).to_broadcast([P, E])).then_inc(s_gate, 16)
            load(Pair(1, 1))
            for k in (2, 3):
                sp.wait_ge(s_x[k % 2], 16)
                load(Pair(k, k % 2))
            with sp.Fori(0, (PAIRS - XBUF) // 2) as n_i:
                i = n_i * 2 + XBUF
                for k in range(2):
                    wait(sp, s_x2, (i + k - XBUF + 1) * NCH)
                    load(Pair(i + k, k))
            sp.wait_ge(s_wz, 1)
            for e in range(E):
                for h in range(2):
                    b = slice(h * C, h * C + C)
                    blocks = lambda at: WALL[b, e, at:at + HC * P].rearrange("p (q m) -> p q m", m=P)[:, :, b]
                    sp.dma_start(blocks(0), w1[e].rearrange("c (q m) -> c q m", m=C)).then_inc(s_wall, 16)
                    sp.dma_start(blocks(W2_AT), w2[e].rearrange("(q m) d -> m q d", m=C)).then_inc(s_wall, 16)
            sp.wait_ge(s_fill, FILLS)
            pad_rows = lambda at: rows[ds(at, SUPER), :].rearrange("(p j) c -> p j c", j=SUB)
            sp.dma_start(pad_rows(IDLE), PAD[:]).then_inc(s_pad, 16)
            sp.wait_ge(s_table, 1)
            for e in range(E):
                end = sp.value_load(endi[0:1, e:e + 1], min_val=e * REGION, max_val=e * REGION + TOKENS)
                sp.dma_start(pad_rows(end), PAD[:]).then_inc(s_pad, 16)
            sp.wait_ge(s_pad, 16 * (E + 1))
            places = [sp.value_load(tbi[0:1, 0, ds(u, 1)], min_val=0, max_val=IDLE) for u in range(RING)]
            for k in range(2):
                for g in range(NG):
                    sp.wait_ge(s_sc[k][g], 16 * scatters[g] * (PAIRS // 2))

            def super_tile(k, u, at=None):
                if at is None:
                    at = sp.value_load(tbi[0:1, 0, ds(k, 1)], min_val=0, max_val=IDLE)
                    wait(sp, s_back[u], (k - u) * (16 * SUB // RING))
                sp.dma_start(RT[:, u], pad_rows(at)).then_inc(s_rt[u], 16)
            for u in range(RING):
                super_tile(u, u, places[u])
            super_tiles(sp, RING, NSUP, super_tile)

            for u in range(RING):
                sp.wait_ge(s_back[u], 16 * SUB * len(range(u, NSUP, RING)))

            def load3(q, odd):
                sp.dma_start(T3(odd), done_v[ds(q, 1)].rearrange("a p m -> (a p) m")).then_inc(s_in3[odd], 16)

            def store3(q, odd):
                wait(sp, s_c3, NG3 * (q + 1))
                sp.dma_start(out_v[ds(q, 1)].rearrange("a p m -> (a p) m"),
                             X[:, odd * HW:odd * HW + HW]).then_inc(s_out[odd], 16)
            load3(0, 0)
            load3(1, 1)
            with sp.Fori(0, (PAIRS - 2) // 2) as n_q:
                q = n_q * 2
                for k in range(2):
                    store3(q + k, k)
                    load3(q + 2 + k, k)
            for k in range(2):
                store3(PAIRS - 2 + k, k)
            for k in range(2):
                sp.wait_ge(s_out[k], 16 * PAIRS // 2)

        @block.tensor
        def _(pe):
            mm = nc.tensor.matmul
            pe.wait_ge(s_fill, FILLS)

            def parameters():
                pe.wait_ge(s_setstep, 1)
                nc.tensor.transpose(PRE[0:P, 0:PROWS], prow[:, :], ident[0:PROWS, 0:PROWS]).then_inc(s_setp, 1)

            def sign_weights():
                pe.wait_ge(s_gate, 48)
                mm(PW[:, GATE_AT:GATE_AT + E], center[:, :], gw2[:, :], start=True, stop=True)
                pe.wait_ge(s_sgn, 4)
                for t0 in range(0, TAPS + 1, GROUP):
                    bk = (CONV[0], CONV[1], PW)[t0 // GROUP]
                    for t in range(t0, min(t0 + GROUP, TAPS + 1)):
                        last = nc.tensor.transpose(bk[:, (t - t0) * P:(t - t0 + 1) * P], SW[:, t, :], ident[:, :])
                    last.then_inc(s_setp, 1)

            def center_chunk(cen, c, alone):
                wait(pe, s_sq, cen.n * NCH + c - alone)
                mm(centered(c, alone)[:, 0:CW], center[:, :], X[:, cen.x(c * CW, CW)],
                   start=True, stop=True).then_inc(s_cen, 1)
                if alone and c == 3:
                    parameters()
                if alone and c == 4:
                    sign_weights()

            def one_pass(cen, nor, con, rou):
                alone = not (nor or con)
                for c in range(NCH):
                    late, j = (con, c - 1) if c else (rou, NCH - 1)
                    norm, jn = (nor, c - 1) if c else (con, NCH - 1)
                    for_rows, rows_slot = (con, c) if c >= 2 else (rou, c + NCH)
                    if cen and c == 0:
                        wait(pe, s_x[cen.odd], (cen.n - cen.odd) * 8 + 16)
                        center_chunk(cen, 0, alone)
                    if con:
                        wait(pe, s_s1, con.n * NCH + min(c + 2, NCH))
                        wait(pe, s_z1, con.n * NCH + c - 1)
                        for t in range(TAPS):
                            dy, dx = t // 3, t % 3
                            last = mm(CONV[(con.odd + c) % 2][:, 0:CW], WB[:, t, :],
                                      S1[:, con.odd, c * CHUNK_ROWS + dy:(c + 1) * CHUNK_ROWS + dy, dx:dx + W],
                                      start=t == 0, stop=t == TAPS - 1)
                        last.then_inc(s_cv, 1)
                    if rou and c == 4:
                        wait(pe, s_oh, rou.n + 1)
                        for e in range(E):
                            last = mm(PRE[0:SLOTS, TOT0 + e:TOT0 + e + 1], onehot[:, :, e], ones[:, 0:1],
                                      start=True, stop=True)
                        last.then_inc(s_tt, 1)
                    if norm:
                        if c == 1:
                            wait(pe, s_r1, norm.n + 1)
                        wait(pe, s_xn, norm.n * NCH + jn)
                        mm(SPREAD[:, 0:CW], pick_bc[:, jn, :], RSTD1[:, :], start=True, stop=True).then_inc(s_bc, 1)
                    if late:
                        wait(pe, s_s2, late.n * NCH + j + 1)
                        wait(pe, s_z2, late.n * NCH + j)
                        mm(PW[:, 0:CW], WB[:, TAPS, :], S2[:, (late.odd + j) % 2, :], start=True, stop=True).then_inc(s_pw, 1)
                    if for_rows:
                        for g in range(NG):
                            if group_slot[g] != rows_slot:
                                continue
                            wait(pe, s_x2, for_rows.n * NCH + last_chunk[g] + 1)
                            before = [b for b in range(g) if second[b] == second[g]]
                            if second[g] and not before:
                                wait(pe, s_rr, for_rows.n)
                            else:
                                wait(pe, s_st, for_rows.n * NG + (before[-1] + 1 if before else 0))
                            for k in group_tiles[g]:
                                at = k % RGROUP * GW
                                last = mm(ROWP[g][:, at:at + GW], X2[:, k * P:(k + 1) * P],
                                          row_weights[:, :], start=True, stop=True)
                            last.then_inc(s_tr, 1)
                    if rou and c == 4:
                        wait(pe, s_of, rou.n + 1)
                        mm(PRE[:, SUM0:SUM0 + E], ones[0:SLOTS, :], tile_tot[:, :], start=True, stop=True)
                        mm(PRE[:, 0:SLOTS * E], upper[:, :], onehot[:].rearrange("p s e -> p (s e)"),
                           start=True, stop=False)
                        mm(PRE[:, 0:SLOTS * E], ones[0:SLOTS, :], tile_off[:].rearrange("p s e -> p (s e)"),
                           start=False, stop=True).then_inc(s_pf, 1)
                    if cen:
                        if c < NCH - 1:
                            center_chunk(cen, c + 1, alone)
                        wait(pe, s_sq, cen.n * NCH + c + 1)
                        if c == 0:
                            wait(pe, s_v1, cen.n)
                        mm(VARP[0:2 * NCH, 0:CW], pick_var[:, c, :], SQ[:, (cen.odd + c) % 2, :],
                           start=c == 0, stop=c == NCH - 1).then_inc(s_vp, 1)
            software_pipeline(pe, one_pass, s_const)

            PT, HA, HV, YT, YB = bank[0:2], bank[2:4], bank[4], bank[5:7], bank[7]

            def super_pass(k, ring, t=True, l1=True, l2=True, back=True):
                if t:
                    b = (ring + 1) % 2
                    wait(pe, s_ln, k + 2)
                    wait_apart(pe, s_xt, k)
                    for d in range(DUO // P):
                        last = nc.tensor.transpose(PT[b][:, d * P:(d + 1) * P],
                                                   XN[:, b, 2 * d:2 * d + 2, :].rearrange("p i c -> p (i c)"), ident[:, :])
                    last.then_inc(s_pt, 1)
                if l1:
                    wait(pe, s_wr, k + 1)
                    wait(pe, s_xt, k + 1)
                    wait(pe, s_ha, k)
                    wait(pe, s_hb, k)
                    for q in range(HC):
                        to = HV[:, 0:DUO] if q == HC - 1 else HA[q // 2][:, (q % 2) * DUO:(q % 2 + 1) * DUO]
                        mm(to, WR[:, ring % WRING, q * P:(q + 1) * P], XT[:, ring % 2, :],
                           start=True, stop=True).then_inc(s_h, 1)
                if l2:
                    b = (ring - 1) % RING
                    wait(pe, s_ha, k)
                    wait(pe, s_hb, k)
                    wait(pe, s_ys, k - 2)
                    for q in range(HC):
                        at = W2_AT + q * P
                        last = mm(YT[b % 2][:, 0:DUO], WR[:, b % WRING, at:at + P], HB[:, b % 2, q, :],
                                  start=q == 0, stop=q == HC - 1)
                    last.then_inc(s_y, 1)
                if back:
                    b = ring % 2
                    wait(pe, s_ys, k - 1)
                    wait_apart(pe, s_g, (k - 3) * GSTEPS + 1)
                    for d in range(DUO // P):
                        last = nc.tensor.transpose(YB[:, d * P:(d + 1) * P], YS[:, b, d * P:(d + 1) * P], ident[:, :])
                    last.then_inc(s_yb, 1)
            super_pass(-1, -1 % RING, l1=False, l2=False, back=False)
            super_pass(0, 0, l2=False, back=False)
            super_pass(1, 1, back=False)
            super_pass(2, 2)
            super_tiles(pe, 3, NSUP - 1, super_pass)
            super_pass(NSUP - 1, (NSUP - 1) % RING, t=False)
            super_pass(NSUP, NSUP % RING, t=False, l1=False)
            super_pass(NSUP + 1, (NSUP + 1) % RING, t=False, l1=False, l2=False)

            def images(q, odd):
                wait(pe, s_in3[odd], (q - odd) * 8 + 16)
                for g in range(NG3):
                    wait(pe, s_c3, (q - 1) * NG3 + g + 1)
                    for j in range(GROUP):
                        t = (g * GROUP + j) * P
                        last = nc.tensor.transpose(bank[g][:, j * PP:(j + 1) * PP],
                                                   T3(odd)[:, t:t + P], ident[0:PP, 0:PP])
                    last.then_inc(s_t3, 1)
            images(0, 0)
            images(1, 1)
            with pe.Fori(0, (PAIRS - 2) // 2) as n_q:
                q = n_q * 2 + 2
                images(q, 0)
                images(q + 1, 1)

        @block.scalar
        def _(act):
            A = nc.scalar.activation
            for h in range(2):
                act.dma_start(W3[h * C:h * C + C, :], w3.rearrange("o i a b -> o (i a b)")).then_inc(s_w, 16)
                act.dma_start(WPW[h * C:h * C + C, :], w_pw.rearrange("o i a b -> o (i a b)")).then_inc(s_w, 16)
            act.wait_ge(s_w, 64)
            A(ABSW[:, :], W3[:, :], ACT.Abs).then_inc(s_absw, 1)
            A(ABSP[:, :], WPW[:, :], ACT.Abs).then_inc(s_absw, 1)
            act.wait_ge(s_zero, 1)
            for h in range(2):
                b = slice(h * C, h * C + C)
                A(SW[b, 0:TAPS, b], W3[b, :].rearrange("o (i t) -> o t i", t=TAPS), ACT.Sign).then_inc(s_sgn, 1)
                A(SW[b, TAPS, b], WPW[b, :], ACT.Sign).then_inc(s_sgn, 1)

            def one_pass(cen, nor, con, rou):
                for c in range(NCH):
                    late, j = (con, c - 1) if c else (rou, NCH - 1)
                    norm, jn = (nor, c - 1) if c else (con, NCH - 1)
                    for_rows, rows_slot = (con, c) if c >= 2 else (rou, c + NCH)
                    if nor and c == 0:
                        wait(act, s_v1, nor.n + 1)
                        A(RA1[:, :], VAR1[:, :], ACT.Abs_reciprocal_sqrt).then_inc(s_sd1, 1)
                    if cen:
                        wait(act, s_cen, cen.n * NCH + c + 1)
                        wait_apart(act, s_x2, (cen.n - ZBUF) * NCH + c + 1)
                        src = centered(c, not (nor or con))[:, 0:CW]
                        A(Z[:, cen.z(c * CW)], src, ACT.Copy).then_inc(s_xc, 1)
                        wait(act, s_vp, cen.n * NCH + c - 1)
                        A(SQ[:, (cen.odd + c) % 2, :], src, ACT.Square).then_inc(s_sq, 1)
                        if not (nor or con) and c == 2:
                            act.wait_ge(s_setstep, VAR_STEP)
                            A(col(TS, 2), col(TA, 2), ACT.Abs_reciprocal_sqrt).then_inc(s_setsd, 1)
                    if norm:
                        wait_apart(act, s_xn, norm.n * NCH + jn + 1)
                        A(S1[:, norm.odd, 1 + jn * CHUNK_ROWS:1 + (jn + 1) * CHUNK_ROWS, 1:1 + W],
                          Z[:, norm.z(jn * CW)].rearrange("p (r w) -> p r w", w=W), ACT.Sign,
                          bias=prm("move1")).then_inc(s_s1, 1)
                    if late:
                        wait_apart(act, s_z2, late.n * NCH + j + 1)
                        A(N2[:, j % 2, :], Z[:, late.z(j * CW)], ACT.Relu, bias=col(NB2P),
                          scale=-1.0).then_inc(s_n2, 1)
                    if con:
                        wait_apart(act, s_q1, con.n * NCH + c + 1)
                        A(S2[:, (con.odd + c) % 2, :], Z[:, con.z(c * CW)], ACT.Sign, bias=col(SG2)).then_inc(s_s2, 1)
                    if rou and c == 2:
                        wait(act, s_rv, rou.n + 1)
                        A(r0[:, :], var2[:, :], ACT.Abs_reciprocal_sqrt).then_inc(s_rs, 1)
                    if rou and c == 3:
                        wait(act, s_sh, rou.n + 1)
                        A(expo[:], shifted[:], ACT.Exp).then_inc(s_ex, 1)
                    if for_rows:
                        r, odd = for_rows.n, for_rows.odd
                        for g in range(NG):
                            if group_slot[g] != rows_slot:
                                continue
                            wait(act, s_tr, r * NG + g + 1)
                            n = len(group_tiles[g])
                            src = ROWP[g][:, 0:n * GW].rearrange("p (k w) -> p k w", w=GW)
                            if g == 0:
                                wait_apart(act, s_rv, r - 1)
                                wait_apart(act, s_lr, r - 1)
                            A(LOGS[:, odd, g * RGROUP:g * RGROUP + n, :], src[:, :, P:GW], ACT.Copy)
                            wait(act, s_sc[odd][g], (r - odd) * 8 * scatters[g])
                            dst = ROWS[:, odd].rearrange("p (h k) r -> p h k r", h=2)
                            whole = g < NG - 1
                            part = [slice(0, P)] * 2 if whole else [slice(0, LAST), slice(LAST, P)]
                            for h in range(2):
                                b = part[h]
                                A(dst[b, h if whole else 0, g * RGROUP:g * RGROUP + n, 0:C],
                                  src[b, :, h * C:h * C + C], ACT.Copy)
                            wait(act, s_st, r * NG + g)
                            for k in range(n):
                                for h in range(2):
                                    slot, b = h * TILES + g * RGROUP + k, part[h]
                                    last = A(SQR[b, 2 * k + h, :], src[b, k, h * C:h * C + C], ACT.Square,
                                             accum_out=SSQ[b, odd, slot:slot + 1])
                            last.then_inc(s_st, 1)
            software_pipeline(act, one_pass, s_const)

            PT, HA, YT = bank[0:2], bank[2:4], bank[5:7]

            def take_weights(k, slot):
                e = act.value_load(tbi[0:1, 1, ds(k, 1)], min_val=0, max_val=E - 1)
                wait_apart(act, s_ys, k - WRING + 1)
                A(WR[:, slot, :], WALL[:, ds(e, 1), :].rearrange("p a w -> p (a w)"), ACT.Copy).then_inc(s_wr, 1)

            def super_pass(k, ring, t=True, h=True, w=True, y=True):
                if t:
                    b = (ring + 1) % 2
                    wait(act, s_pt, k + 2)
                    wait(act, s_h, HC * k)
                    A(XT[:, b, :], PT[b][:, 0:DUO], ACT.Copy).then_inc(s_xt, 1)
                if h:
                    wait(act, s_y, k - 1)
                    for q in range(HC - 1):
                        wait(act, s_h, HC * k + min(q // 2 * 2 + 2, HC - 1))
                        last = A(HB[:, ring % 2, q, :], HA[q // 2][:, (q % 2) * DUO:(q % 2 + 1) * DUO], ACT.Relu,
                                 bias=WR[:, ring % WRING, B1_AT + q:B1_AT + q + 1])
                    last.then_inc(s_ha, 1)
                if w:
                    take_weights(k + 2, (ring + 2) % WRING)
                if y:
                    b = (ring - 1) % RING
                    wait(act, s_y, k)
                    wait_apart(act, s_yb, k - 2)
                    A(YS[:, b % 2, :], YT[b % 2][:, 0:DUO], ACT.Identity,
                      bias=WR[:, b % WRING, B2_AT:B2_AT + 1]).then_inc(s_ys, 1)
            act.wait_ge(s_wall, 16 * 4 * E)
            act.wait_ge(s_table, 1)
            take_weights(0, 0)
            super_pass(-1, -1 % RING, h=False, y=False)
            super_pass(0, 0, y=False)
            super_pass(1, 1)
            super_pass(2, 2)
            super_tiles(act, 3, NSUP - 2, super_pass)
            super_pass(NSUP - 2, (NSUP - 2) % RING, w=False)
            super_pass(NSUP - 1, (NSUP - 1) % RING, t=False, w=False)
            super_pass(NSUP, NSUP % RING, t=False, h=False, w=False)

            def copy_images(q, odd):
                wait(act, s_out[odd], (q - odd) * 8)
                for g in range(NG3):
                    wait(act, s_t3, q * NG3 + g + 1)
                    dst = X[:, odd * HW:odd * HW + HW].rearrange("p (t j) -> p j t", j=PJ)
                    A(dst[:, g * GROUP:(g + 1) * GROUP, :],
                      bank[g][:, 0:GROUP * PP].rearrange("p (j t) -> p j t", t=PP), ACT.Copy).then_inc(s_c3, 1)
            copy_images(0, 0)
            copy_images(1, 1)
            with act.Fori(0, PAIRS // 2 - 1) as n:
                copy_images(n * 2 + 2, 0)
                copy_images(n * 2 + 3, 1)

        @block.vector
        def _(dve):
            V = nc.vector
            n = [0]

            def step(ins):
                n[0] += 1
                ins.then_inc(s_setstep, 1)
                dve.wait_ge(s_setstep, n[0])
            V.memset(SW[:], 0.0).then_inc(s_zero, 1)
            V.memset(S1[:].bitcast(u32), 0)
            for e in range(E):
                V.memset(region0[:, e:e + 1], float(e * REGION - 1))
            dve.wait_ge(s_param, 16 * (NPAR + 2))
            step(V.tensor_copy(prow[:, C:P], prow[:, 0:C]))
            dve.wait_ge(s_setp, 1)
            step(V.tensor_copy(par[:, :], PRE[:, 0:PROWS]))
            step(V.tensor_scalar(col(TA, 2), prm("va1", 2), EPS_BN, None, ALU.add))
            assert n[0] == VAR_STEP
            step(V.tensor_copy(base[:, :], region0[:, :]))
            dve.wait_ge(s_absw, 2)
            step(V.tensor_reduce(col(ABSM), ABSW[:, :], AX.X, ALU.add))
            step(V.tensor_reduce(col(ABSM + 1), ABSP[:, :], AX.X, ALU.add))
            step(V.tensor_scalar(col(ABSM), col(ABSM), 1.0 / (C * TAPS), None, ALU.mult))
            step(V.tensor_scalar(col(ABSM + 1), col(ABSM + 1), 1.0 / C, None, ALU.mult))
            dve.wait_ge(s_setsd, 1)
            step(V.tensor_tensor(col(TBB, 2), col(TS, 2), col(TS, 2), ALU.mult))
            step(V.scalar_tensor_tensor(out=col(TBB, 2), in0=col(TBB, 2), scalar=-0.5, in1=col(TA, 2), op0=ALU.mult, op1=ALU.mult))
            step(V.scalar_tensor_tensor(out=col(TS, 2), in0=col(TBB, 2), scalar=1.5, in1=col(TS, 2), op0=ALU.add, op1=ALU.mult))
            step(V.tensor_tensor(col(INV, 2), col(TS, 2), prm("g1", 2), ALU.mult))
            step(V.tensor_tensor(col(S_, 2), col(INV, 2), col(ABSM, 2), ALU.mult))
            step(V.tensor_tensor(col(BIAS, 2), prm("mu1", 2), col(INV, 2), ALU.mult))
            step(V.tensor_tensor(col(BIAS, 2), prm("be1", 2), col(BIAS, 2), ALU.subtract))
            step(V.tensor_scalar(col(SM1), prm("ps1"), -1.0, None, ALU.add))
            step(V.tensor_scalar(col(OMS), prm("ps2"), -1.0, 1.0, ALU.mult, ALU.add))
            step(V.tensor_tensor(col(B1P), col(BIAS), prm("pm1"), ALU.add))
            step(V.tensor_tensor(col(CA), col(B1P), prm("pb1"), ALU.add))
            step(V.tensor_tensor(col(SG2), col(CA), prm("move2"), ALU.add))
            step(V.tensor_tensor(col(B2P), col(BIAS + 1), col(CA), ALU.add))
            step(V.tensor_tensor(col(B2P), col(B2P), prm("pm2"), ALU.add))
            step(V.tensor_scalar(col(NB2P), col(B2P), -1.0, None, ALU.mult))
            step(V.tensor_tensor(col(CB), col(B2P), prm("pb2"), ALU.add))
            dve.wait_ge(s_setp, 4)
            dve.wait_ge(s_fill, FILLS)
            for h in range(2):
                step(V.tensor_copy(gate[h * C:h * C + C, h * E:h * E + E], PW[h * C:h * C + C, GATE_AT:GATE_AT + E]))
                step(V.memset(gate[h * C:h * C + C, ME + h:ME + h + 1], 1.0 / C))
            for t0 in range(0, TAPS + 1, GROUP):
                t1 = min(t0 + GROUP, TAPS + 1)
                bk = (CONV[0], CONV[1], PW)[t0 // GROUP]
                step(V.tensor_copy(WB[:, t0:t1, :], bk[:, 0:(t1 - t0) * P].rearrange("p (t m) -> p t m", m=P)))
            V.memset(SSQ[:], 1.0).then_inc(s_const, 1)

            over = lambda ap, m: ap.unsqueeze(1).to_broadcast([P, SLOTS, m])
            spread = lambda ap: ap.unsqueeze(2).to_broadcast([P, SLOTS, E])
            flat = lambda t: t[:].rearrange("p s e -> p (s e)")
            def route(p, c):
                r = [ROUTE_AT[c]]

                def op(ins, s=None):
                    if s is not None:
                        ins.then_inc(s, 1)
                        return
                    r[0] += 1
                    ins.then_inc(s_route, 1)
                    wait(dve, s_route, p.n * NROUTE + r[0])
                if c == 0:
                    wait(dve, s_st, (p.n + 1) * NG)
                    V.tensor_copy(ROWS[:, p.odd, :, MEAN].rearrange("p (h k) -> p h k", h=2),
                                  LOGS[:, p.odd, :, ME:ME + 2].rearrange("p k h -> p h k"))
                    op(V.tensor_scalar(var2[:], SSQ[:, p.odd], 1.0 / C, EPS_T, ALU.mult, ALU.add), s_rv)
                if c == 1:
                    wait(dve, s_rs, p.n + 1)
                    op(V.tensor_tensor(ra[:], r0[:], r0[:], ALU.mult))
                    op(V.scalar_tensor_tensor(out=rb[:], in0=ra[:], scalar=-0.5, in1=var2[:], op0=ALU.mult, op1=ALU.mult))
                    rstd = ROWS[:, p.odd, :, RSTD]
                    op(V.scalar_tensor_tensor(out=rstd, in0=rb[:], scalar=1.5, in1=r0[:], op0=ALU.add, op1=ALU.mult))
                    for h in range(2):
                        sl = slice(h * TILES, (h + 1) * TILES)
                        ins = V.tensor_tensor(
                            logit[:, sl, :], LOGS[:, p.odd, :, h * E:h * E + E],
                            ROWS[:, p.odd, sl, RSTD:RSTD + 1].to_broadcast([P, TILES, E]), ALU.mult)
                    ins.then_inc(s_lr, 1)
                    wait(dve, s_lr, p.n + 1)
                    op(V.tensor_tensor(logit[:], logit[:], over(gb[:, :], E), ALU.add))
                    op(V.tensor_reduce(mx[:], logit[:], AX.X, ALU.max))
                    op(V.tensor_tensor(shifted[:], logit[:], spread(mx[:]), ALU.subtract), s_sh)
                if c == 2:
                    wait(dve, s_sh, p.n + 1)
                    op(V.scalar_tensor_tensor(out=cand[:], in0=shifted[:], scalar=0.0, in1=over(iota8[:, :], E),
                                              op0=ALU.is_ge, op1=ALU.mult))
                    op(V.tensor_reduce(imin[:], cand[:], AX.X, ALU.min))
                    op(V.tensor_tensor(onehot[:], over(iota8[:, :], E), spread(imin[:]), ALU.is_equal))
                    V.memset(onehot[LAST:P, TILES - 1, :], 0.0)
                    op(V.memset(onehot[0:LAST, SLOTS - 1, :], 0.0), s_oh)
                    wait(dve, s_ex, p.n + 1)
                    op(V.tensor_reduce(ssum[:], expo[:], AX.X, ALU.add))
                    op(V.reciprocal(prob[:], ssum[:]))
                if c == 3:
                    wait(dve, s_tt, p.n + 1)
                    op(V.tensor_copy(tile_tot[:, :], PRE[0:SLOTS, TOT0:TOT0 + E]))
                    op(V.tensor_tensor(tile_off[:], earlier[:, :].unsqueeze(2).to_broadcast([SLOTS, SLOTS, E]),
                                       tile_tot[:, :].unsqueeze(1).to_broadcast([SLOTS, SLOTS, E]), ALU.mult), s_of)
                if c == 4:
                    wait(dve, s_pf, p.n + 1)
                    op(V.tensor_tensor(rowsel[:], PRE[:, 0:SLOTS * E].rearrange("p (s e) -> p s e", e=E),
                                       over(base[:, :], E), ALU.add))
                    op(V.tensor_tensor(base[:, :], base[:, :], PRE[:, SUM0:SUM0 + E], ALU.add))
                    op(V.tensor_tensor(rowsel[:], rowsel[:], onehot[:], ALU.mult))
                    op(V.tensor_reduce(rowid[:], rowsel[:], AX.X, ALU.add))
                    V.tensor_copy(idx[:, p.odd, :], rowid[:])
                    op(V.scalar_tensor_tensor(out=posn[:], in0=imin[:], scalar=-float(REGION), in1=rowid[:],
                                              op0=ALU.mult, op1=ALU.add))
                    V.tensor_copy(idx[LAST:P, p.odd, TILES - 1:TILES], rowid[LAST:P, SLOTS - 1:SLOTS])
                    V.tensor_copy(ROWS[:, p.odd, :, TOKEN].bitcast(u32), tokf[:])
                    op(V.scalar_tensor_tensor(out=ROWS[:, p.odd, :, GATE], in0=posn[:], scalar=float(E * REGION + CAPACITY),
                                              in1=prob[:], op0=ALU.is_lt, op1=ALU.mult))
                    V.tensor_scalar(tokf[:], tokf[:], float(2 * HW), None, ALU.add)
                    V.tensor_copy(ROWS[LAST:P, p.odd, TILES - 1, MEAN:ROW],
                                  ROWS[LAST:P, p.odd, SLOTS - 1, MEAN:ROW]).then_inc(s_rr, 1)
                assert r[0] == ROUTE_AT[c + 1]

            def one_pass(cen, nor, con, rou):
                for c in range(NCH):
                    late, j = (con, c - 1) if c else (rou, NCH - 1)
                    norm, jn = (nor, c - 1) if c else (con, NCH - 1)
                    for_rows, rows_slot = (con, c) if c >= 2 else (rou, c + NCH)
                    first = nor and c == 0
                    if first:
                        wait(dve, s_vp, (nor.n + 1) * NCH)
                        V.tensor_scalar(VAR1[:, :], VARP[0:2 * NCH, 0:CW], EPS_C, None, ALU.add).then_inc(s_v1, 1)
                    if con:
                        wait(dve, s_cv, con.n * NCH + c + 1)
                        z = Z[:, con.z(c * CW)]
                        V.scalar_tensor_tensor(out=z, in0=CONV[(con.odd + c) % 2][:, 0:CW], scalar=col(S_), in1=z,
                                               op0=ALU.mult, op1=ALU.add).then_inc(s_z1, 1)
                    if norm:
                        wait(dve, s_bc, norm.n * NCH + jn + 1)
                        wait(dve, s_xc, norm.n * NCH + jn + 1)
                        z = Z[:, norm.z(jn * CW)]
                        V.tensor_tensor(z, z, SPREAD[:, 0:CW], ALU.mult).then_inc(s_xn, 1)
                    if rou and c == 2:
                        route(rou, 0)
                    if first:
                        wait(dve, s_sd1, nor.n + 1)
                        V.tensor_tensor(RB1[:, :], RA1[:, :], RA1[:, :], ALU.mult).then_inc(s_nw, 1)
                    if con:
                        wait(dve, s_z1, con.n * NCH + c + 1)
                        V.tensor_scalar(N1[:, c % 2, :], Z[:, con.z(c * CW)], col(B1P), 0.0,
                                        ALU.add, ALU.min).then_inc(s_n1, 1)
                    if first:
                        wait(dve, s_nw, nor.n * 2 + 1)
                        V.scalar_tensor_tensor(out=RB1[:, :], in0=RB1[:, :], scalar=-0.5, in1=VAR1[:, :],
                                               op0=ALU.mult, op1=ALU.mult).then_inc(s_nw, 1)
                    if late:
                        wait(dve, s_pw, late.n * NCH + j + 1)
                        z = Z[:, late.z(j * CW)]
                        V.scalar_tensor_tensor(out=z, in0=PW[:, 0:CW], scalar=col(S_ + 1), in1=z,
                                               op0=ALU.mult, op1=ALU.add).then_inc(s_z2, 1)
                    if con:
                        wait(dve, s_n1, con.n * NCH + c + 1)
                        z = Z[:, con.z(c * CW)]
                        V.scalar_tensor_tensor(out=z, in0=N1[:, c % 2, :], scalar=col(SM1), in1=z,
                                               op0=ALU.mult, op1=ALU.add).then_inc(s_q1, 1)
                    if first:
                        wait(dve, s_nw, nor.n * 2 + 2)
                        wait(dve, s_bc, nor.n * NCH)
                        V.scalar_tensor_tensor(out=RSTD1[:, :], in0=RB1[:, :], scalar=1.5, in1=RA1[:, :],
                                               op0=ALU.add, op1=ALU.mult).then_inc(s_r1, 1)
                    if rou and c in (3, 4):
                        route(rou, c - 1)
                    if late:
                        wait(dve, s_n2, late.n * NCH + j + 1)
                        z = Z[:, late.z(j * CW)]
                        V.scalar_tensor_tensor(out=z, in0=N2[:, j % 2, :], scalar=col(OMS), in1=z,
                                               op0=ALU.mult, op1=ALU.add).then_inc(s_q2, 1)
                        wait(dve, s_q2, late.n * NCH + j + 1)
                        old = next(g for g in range(NG) if last_chunk[g] >= j and (g + 1) * RGROUP * P >= (j + 1) * CW
                                   or g == NG - 1)
                        wait(dve, s_tr, (late.n - 1) * NG + old + 1)
                        if j == NCH - 1:
                            V.scalar_tensor_tensor(out=X2[:, HW:HW + LAST], in0=Z[:, late.z(HW - LAST, LAST)],
                                                   scalar=col(CB), in1=X[:, late.x(HW - LAST, LAST)],
                                                   op0=ALU.add, op1=ALU.add)
                        V.scalar_tensor_tensor(out=X2[:, j * CW:(j + 1) * CW], in0=z, scalar=col(CB),
                                               in1=X[:, late.x(j * CW, CW)], op0=ALU.add, op1=ALU.add).then_inc(s_x2, 1)
                    if rou and c == 2:
                        route(rou, 1)
                    if rou and c == 4:
                        route(rou, 4)
            software_pipeline(dve, one_pass)

            m = [0]

            def tstep(ins):
                m[0] += 1
                ins.then_inc(s_tab, 1)
                dve.wait_ge(s_tab, m[0])
            dve.wait_ge(s_x2, PAIRS * NCH)
            tstep(V.memset(WALL[:], 0.0))
            tstep(V.tensor_copy(WALL[:, :, B1_AT:B1_AT + HC],
                                par[:, NPAR:NPAR + E * HC].rearrange("p (e q) -> p e q", q=HC)))
            V.tensor_copy(WALL[:, :, B2_AT], par[:, NPAR + E * HC:PROWS]).then_inc(s_wz, 1)
            dve.wait_ge(s_rr, PAIRS)
            tstep(V.tensor_scalar(ends[:, :], base[0:1, :], 1.0, None, ALU.add))
            tstep(V.tensor_copy(endi[:, :], ends[:, :]))
            tstep(V.tensor_tensor(ntf[:, :], base[0:1, :], region0[0:1, :], ALU.subtract))
            tstep(V.tensor_scalar(ntf[:, :], ntf[:, :], float(SUPER - 1), None, ALU.add))
            tstep(V.tensor_copy(nti[:, :], ntf[:, :]))
            tstep(V.tensor_scalar(nti[:, :], nti[:, :], SUPER.bit_length() - 1, None, ALU.arith_shift_right))
            tstep(V.tensor_copy(ntf[:, :], nti[:, :]))
            tstep(V.tensor_copy(ntp[:, :], ntf[:, :]))
            for e in range(1, E):
                tstep(V.tensor_tensor(ntp[:, e:e + 1], ntp[:, e:e + 1], ntp[:, e - 1:e], ALU.add))
            tstep(V.tensor_scalar(ntd[:, :], ntf[:, :], -float(SUPER), float(REGION), ALU.mult, ALU.add))
            tstep(V.tensor_scalar(tb[:, 0, :], kio[:, :], float(SUPER), None, ALU.mult))
            tstep(V.memset(tb[:, 1, :], 0.0))
            for e in range(E):
                tstep(V.tensor_scalar(ind[:, :], kio[:, :], ntp[:, e:e + 1], ntd[:, e:e + 1], ALU.is_ge, ALU.mult))
                tstep(V.tensor_tensor(tb[:, 0, :], tb[:, 0, :], ind[:, :], ALU.add))
                tstep(V.scalar_tensor_tensor(out=tb[:, 1, :], in0=kio[:, :], scalar=ntp[:, e:e + 1], in1=tb[:, 1, :],
                                             op0=ALU.is_ge, op1=ALU.add))
            tstep(V.tensor_scalar(tbe[:, 0, :], tb[:, 0, :], float(IDLE), None, ALU.min))
            tstep(V.tensor_scalar(tbe[:, 1, :], tb[:, 1, :], float(E - 1), None, ALU.min))
            V.tensor_copy(tbi[:], tbe[:]).then_inc(s_table, 1)

            HV, YB = bank[4], bank[7]

            def super_pass(k, ring, ln=True, h=True, fin=True):
                if ln:
                    u, b = (ring + 2) % RING, ring % 2
                    wait(dve, s_rt[u], (k + 2 - u) * (16 // RING) + 16)
                    wait(dve, s_pt, k + 1)
                    V.tensor_tensor(XN[:, b], RT[:, u, :, 0:C], RT[:, u, :, RSTD:RSTD + 1].to_broadcast([P, SUB, C]),
                                    ALU.mult).then_inc(s_ln, 1)
                if h:
                    wait(dve, s_h, HC * k + HC)
                    wait(dve, s_y, k - 1)
                    q = HC - 1
                    V.tensor_scalar(HB[:, ring % 2, q, :], HV[:, 0:DUO], WR[:, ring % WRING, B1_AT + q:B1_AT + q + 1],
                                    0.0, ALU.add, ALU.max).then_inc(s_hb, 1)
                if fin:
                    u = (ring - 2) % RING
                    g = [0]

                    def gstep(ins, wait=wait):
                        g[0] += 1
                        ins.then_inc(s_g, 1)
                        wait(dve, s_g, (k - 2) * GSTEPS + g[0])
                    wait(dve, s_yb, k - 1)
                    y = YB[:, 0:SUB * C].rearrange("p (j c) -> p j c", c=C)
                    gstep(V.tensor_tensor(Y2[:], y, RT[:, u, :, GATE:GATE + 1].to_broadcast([P, SUB, C]), ALU.mult))
                    V.tensor_tensor(TOKS[:], RT[:, u, :, 0:C], RT[:, u, :, MEAN:MEAN + 1].to_broadcast([P, SUB, C]), ALU.add)
                    V.tensor_scalar(FINITE[:], Y2[:], 0.0, 0.0, ALU.mult, ALU.is_equal)
                    gstep(V.tensor_scalar(SGN[:], Y2[:], 0.0, None, ALU.is_gt))
                    gstep(V.scalar_tensor_tensor(out=SGN[:], in0=Y2[:], scalar=0.0, in1=SGN[:], op0=ALU.is_lt, op1=ALU.subtract))
                    gstep(V.tensor_scalar(Y3[:], SGN[:], -LIMIT, None, ALU.mult), wait_apart)
                    gstep(V.copy_predicated(Y3[:], FINITE[:], Y2[:]))
                    assert g[0] == GSTEPS
                    V.tensor_tensor(RES[:, u], Y3[:], TOKS[:], ALU.add).then_inc(s_res, 1)
            super_pass(-2, -2 % RING, h=False, fin=False)
            super_pass(-1, -1 % RING, h=False, fin=False)
            super_pass(0, 0, fin=False)
            super_pass(1, 1, fin=False)
            super_pass(2, 2)
            super_tiles(dve, 3, NSUP - 2, super_pass)
            super_pass(NSUP - 2, (NSUP - 2) % RING, ln=False)
            super_pass(NSUP - 1, (NSUP - 1) % RING, ln=False)
            super_pass(NSUP, NSUP % RING, ln=False, h=False)
            super_pass(NSUP + 1, (NSUP + 1) % RING, ln=False, h=False)


_INS = ['x', 'L0_conv_move1_bias', 'L0_conv_w3', 'L0_conv_bn1_gamma', 'L0_conv_bn1_beta', 'L0_conv_bn1_mean',
        'L0_conv_bn1_var', 'L0_conv_prelu1_move', 'L0_conv_prelu1_slope', 'L0_conv_prelu1_bias', 'L0_conv_move2_bias',
        'L0_conv_w_pw', 'L0_conv_bn2_gamma', 'L0_conv_bn2_beta', 'L0_conv_bn2_mean', 'L0_conv_bn2_var',
        'L0_conv_prelu2_move', 'L0_conv_prelu2_slope', 'L0_conv_prelu2_bias', 'L0_ffn_gate_w', 'L0_ffn_gate_b',
        'L0_ffn_w1', 'L0_ffn_b1', 'L0_ffn_w2', 'L0_ffn_b2']


def kernel(**inputs):
    import numpy as _np
    import concourse.bacc as _bacc
    from concourse import mybir as _mybir
    from concourse.bass_utils import run_bass_kernel_spmd as _run

    nc = _bacc.Bacc("TRN2", target_bir_lowering=False, num_devices=1)
    arrays, args = {}, []
    for name in _INS:
        a = _np.ascontiguousarray(inputs[name])
        arrays[f"in_{name}_dram"] = a
        args.append(nc.dram_tensor(f"in_{name}_dram", a.shape, _mybir.dt.from_np(a.dtype), kind="ExternalInput").ap())
    shape = inputs['x'].shape
    args.append(nc.dram_tensor("out_0_dram", shape, _mybir.dt.float32, kind="ExternalOutput").ap())
    metaformer_kernel(nc, *args)
    r = _run(nc, [arrays], core_ids=[0])
    return r.results[0]["out_0_dram"]
```
